# Optimizing a Trainium2 kernel written in Bass

```python
import numpy as np
import jax
import jax.numpy as jnp

def _softmax(x, axis=-1):
    return jax.nn.softmax(x, axis=axis)

def _gelu(x):
    return jax.nn.gelu(x, approximate=True)

def _silu(x):
    return jax.nn.silu(x)

def _sigmoid(x):
    return jax.nn.sigmoid(x)

def _layernorm(x, axis=-1, eps=1e-05):
    m = jnp.mean(x, axis=axis, keepdims=True)
    v = jnp.var(x, axis=axis, keepdims=True)
    return (x - m) / jnp.sqrt(v + eps)

def _scatter_add(tgt, idx, src, axis=0):
    return tgt.at[idx].add(src)

def _segment_sum(src, seg, n):
    return jax.ops.segment_sum(src, seg, n)
kernel_name = 'mk_early_fusion_embed_d1_tok_img256_r4_84b7fb'

def setup_inputs(seed: int=0):
    np.random.seed(seed)
    _w = jnp.asarray

    def _rec_inputs():
        import jax
        import jax.numpy as jnp
        _rk = jax.random.key(seed)
        x = -0.000222058 + 0.999998 * jax.random.normal(jax.random.fold_in(_rk, 1), (64, 3, 96, 96), jnp.float32)
        x_txt = jax.random.randint(jax.random.fold_in(_rk, 51), (64, 77), 0, 64, jnp.int32)
        return (x, x_txt)
    x, x_txt = _rec_inputs()

    def _L0_tok_setup():
        import jax, jax.numpy as jnp
        import numpy as np
        IMAGE_SIZE = 64
        PATCH = 16
        EMBED_DIM = 64
        IN_CH = 3
        BATCH = 128
        IN_DIM = IN_CH * PATCH * PATCH

        def _patchify(x, p):
            B, C, H, Wd = x.shape
            x = x.reshape(B, C, H // p, p, Wd // p, p)
            x = x.transpose(0, 2, 4, 1, 3, 5)
            return x.reshape(B, H // p * (Wd // p), C * p * p)
        key = jax.random.key(seed)
        kx, kw, kb = jax.random.split(key, 3)
        x = jax.random.normal(kx, (BATCH, IN_CH, IMAGE_SIZE, IMAGE_SIZE), dtype=jnp.float32)
        W = jax.random.normal(kw, (EMBED_DIM, IN_DIM), dtype=jnp.float32) * (1.0 / np.sqrt(IN_DIM))
        b = jax.random.normal(kb, (EMBED_DIM,), dtype=jnp.float32) * 0.01
        return {'x': x, 'W': W, 'b': b}
    _L0_tok_all = _L0_tok_setup()
    _L0_tok_in = {k: v for k, v in _L0_tok_all.items() if k in ('W', 'b')}
    del _L0_tok_all

    def _L0_txt_setup():
        import jax, jax.numpy as jnp
        import numpy as np
        D_MODEL = 128
        N_LAYERS = 4
        VOCAB = 64
        SEQ = 512
        BATCH = 8
        EPS = 1e-05

        def _ln(x, g, b):
            mu = jnp.mean(x, axis=-1, keepdims=True)
            var = jnp.mean(jnp.square(x - mu), axis=-1, keepdims=True)
            return (x - mu) * jax.lax.rsqrt(var + EPS) * g + b

        def _fast_memory(x, mask, W_upd, b_upd, W_f, b_f, decay_param):
            decay = jax.nn.sigmoid(decay_param[0])
            u = jnp.einsum('bsd,de->bse', x, W_upd) + b_upd
            u_t = jnp.swapaxes(u, 0, 1)
            m_t = jnp.swapaxes(mask, 0, 1)[..., None]

            def step(mem, inp):
                u_i, msk = inp
                new = decay * mem + u_i
                mem = msk * new + (1.0 - msk) * mem
                return (mem, mem)
            mem0 = jnp.zeros((x.shape[0], x.shape[2]), x.dtype)
            _, mems = jax.lax.scan(step, mem0, (u_t, m_t))
            mems = jnp.swapaxes(mems, 0, 1)
            return jnp.einsum('bsd,de->bse', mems, W_f) + b_f
        key = jax.random.key(seed)
        ks = jax.random.split(key, 16)
        d, dff = (D_MODEL, 4 * D_MODEL)
        s = 0.02
        inp = {'tokens': jax.random.randint(ks[0], (BATCH, SEQ), 0, VOCAB, dtype=jnp.int64), 'emb': jax.random.normal(ks[1], (VOCAB, d), jnp.float32) * s, 'W_upd': jax.random.normal(ks[2], (d, d), jnp.float32) * s, 'b_upd': jnp.zeros((d,), jnp.float32), 'W_f': jax.random.normal(ks[3], (d, d), jnp.float32) * s, 'b_f': jnp.zeros((d,), jnp.float32), 'decay_param': jnp.zeros((1,), jnp.float32), 'norm_g': jnp.ones((d,), jnp.float32), 'norm_b': jnp.zeros((d,), jnp.float32), 'cms_ln_g': jnp.ones((N_LAYERS, d), jnp.float32), 'cms_ln_b': jnp.zeros((N_LAYERS, d), jnp.float32), 'cms_W1': jax.random.normal(ks[4], (N_LAYERS, d, dff), jnp.float32) * s, 'cms_b1': jnp.zeros((N_LAYERS, dff), jnp.float32), 'cms_W2': jax.random.normal(ks[5], (N_LAYERS, dff, d), jnp.float32) * s, 'cms_b2': jnp.zeros((N_LAYERS, d), jnp.float32), 'head_W': jax.random.normal(ks[6], (d, VOCAB), jnp.float32) * s, 'head_b': jnp.zeros((VOCAB,), jnp.float32)}
        return inp
    _L0_txt_all = _L0_txt_setup()
    _L0_txt_in = {k: v for k, v in _L0_txt_all.items() if k in ('emb', 'W_upd', 'b_upd', 'W_f', 'b_f', 'decay_param', 'norm_g', 'norm_b', 'cms_ln_g', 'cms_ln_b', 'cms_W1', 'cms_b1', 'cms_W2', 'cms_b2', 'head_W', 'head_b')}
    del _L0_txt_all

    def _L0_attn_setup():
        import jax, jax.numpy as jnp
        from jax import lax
        import numpy as np
        D_MODEL = 64
        D_INNER = 128
        D_STATE = 16
        D_CONV = 4
        DT_RANK = 16
        B = 2
        T = 1024

        def _mamba(x, W_in, conv_w, conv_b, W_x, W_dt, b_dt, A_log, D, W_out):
            b, t, _ = x.shape
            xz = x @ W_in
            xi, z = jnp.split(xz, 2, axis=-1)
            xc = lax.conv_general_dilated(xi.transpose(0, 2, 1), conv_w[:, None, :], (1,), [(D_CONV - 1, 0)], dimension_numbers=('NCH', 'OIH', 'NCH'), feature_group_count=D_INNER)
            xi = jax.nn.silu(xc.transpose(0, 2, 1) + conv_b)
            xdbl = xi @ W_x
            dt, Bm, Cm = jnp.split(xdbl, [DT_RANK, DT_RANK + D_STATE], axis=-1)
            dt = jax.nn.softplus(dt @ W_dt + b_dt)
            A = -jnp.exp(A_log)
            dA = jnp.exp(dt[..., None] * A)
            dBx = dt[..., None] * Bm[:, :, None, :] * xi[..., None]

            def step(h, ins):
                dA_t, dBx_t, C_t = ins
                h = dA_t * h + dBx_t
                y = jnp.einsum('bdn,bn->bd', h, C_t)
                return (h, y)
            h0 = jnp.zeros((b, D_INNER, D_STATE), x.dtype)
            _, ys = lax.scan(step, h0, (dA.transpose(1, 0, 2, 3), dBx.transpose(1, 0, 2, 3), Cm.transpose(1, 0, 2)))
            y = ys.transpose(1, 0, 2) + xi * D
            y = y * jax.nn.silu(z)
            return y @ W_out

        def _mamba_params(key, prefix):
            ks = jax.random.split(key, 6)
            s = 0.02
            return {prefix + '_W_in': jax.random.normal(ks[0], (D_MODEL, 2 * D_INNER)) * s, prefix + '_conv_w': jax.random.normal(ks[1], (D_INNER, D_CONV)) * s, prefix + '_conv_b': jnp.zeros((D_INNER,), jnp.float32), prefix + '_W_x': jax.random.normal(ks[2], (D_INNER, DT_RANK + 2 * D_STATE)) * s, prefix + '_W_dt': jax.random.normal(ks[3], (DT_RANK, D_INNER)) * s, prefix + '_b_dt': jax.random.normal(ks[4], (D_INNER,)) * s, prefix + '_A_log': jnp.log(jnp.tile(jnp.arange(1, D_STATE + 1, dtype=jnp.float32), (D_INNER, 1))), prefix + '_D': jnp.ones((D_INNER,), jnp.float32), prefix + '_W_out': jax.random.normal(ks[5], (D_INNER, D_MODEL)) * s}
        key = jax.random.key(seed)
        kx, kf, kb, km = jax.random.split(key, 4)
        inp = {'x': jax.random.normal(kx, (B, T, D_MODEL), jnp.float32)}
        inp.update(_mamba_params(kf, 'fw'))
        inp.update(_mamba_params(kb, 'bw'))
        inp['merge_W'] = jax.random.normal(km, (2 * D_MODEL, D_MODEL)) * 0.02
        return inp
    _L0_attn_all = _L0_attn_setup()
    _L0_attn_in = {k: v for k, v in _L0_attn_all.items() if k in ('fw_W_in', 'fw_conv_w', 'fw_conv_b', 'fw_W_x', 'fw_W_dt', 'fw_b_dt', 'fw_A_log', 'fw_D', 'fw_W_out', 'bw_W_in', 'bw_conv_w', 'bw_conv_b', 'bw_W_x', 'bw_W_dt', 'bw_b_dt', 'bw_A_log', 'bw_D', 'bw_W_out', 'merge_W')}
    del _L0_attn_all

    def _L0_ffn_setup():
        import jax, jax.numpy as jnp
        import numpy as np
        DIM = 64
        HEADS = 8
        NUM_KEYS = 64
        NUM_KV = NUM_KEYS ** 2
        PK_TOPK = 16
        FINAL_TOPK = 16
        DIM_KEY = DIM // 2
        P = 2

        def _pk(x, Wq_pk, pk_keys):
            b, n, _ = x.shape
            q = (x @ Wq_pk).reshape(b, n, P, HEADS, DIM_KEY).transpose(2, 0, 1, 3, 4)
            sim = jnp.einsum('pbnhd,pkhd->pbnhk', q, pk_keys)
            scores, idx = jax.lax.top_k(sim, PK_TOPK)
            idx0 = idx[0]
            idx1 = idx[1] * NUM_KEYS
            index = (idx0[..., :, None] + idx1[..., None, :]).reshape(b, n, HEADS, PK_TOPK * PK_TOPK)
            score = (scores[0][..., :, None] + scores[1][..., None, :]).reshape(b, n, HEADS, PK_TOPK * PK_TOPK)
            final_scores, pk_idx = jax.lax.top_k(score, FINAL_TOPK)
            final_indices = jnp.take_along_axis(index, pk_idx, axis=-1)
            final_scores = jax.nn.softmax(final_scores, axis=-1)
            return (final_scores, final_indices)
        key = jax.random.key(seed)
        ks = jax.random.split(key, 7)
        b, n = (2, 256)
        std = 0.02
        x = jax.random.normal(ks[0], (b, n, DIM), dtype=jnp.float32)
        Wq_pk = jax.random.normal(ks[1], (DIM, P * HEADS * DIM_KEY), dtype=jnp.float32) * std
        pk_keys = jax.random.normal(ks[2], (P, NUM_KEYS, HEADS, DIM_KEY), dtype=jnp.float32) * std
        Wq = jax.random.normal(ks[3], (DIM, HEADS * DIM), dtype=jnp.float32) * std
        keys_table = jax.random.normal(ks[4], (NUM_KV * HEADS, DIM), dtype=jnp.float32) * std
        values_table = jax.random.normal(ks[5], (NUM_KV * HEADS, DIM), dtype=jnp.float32) * std
        Wo = jax.random.normal(ks[6], (DIM * HEADS, DIM), dtype=jnp.float32) * std
        return {'x': x, 'Wq_pk': Wq_pk, 'pk_keys': pk_keys, 'Wq': Wq, 'keys_table': keys_table, 'values_table': values_table, 'Wo': Wo}
    _L0_ffn_all = _L0_ffn_setup()
    _L0_ffn_in = {k: v for k, v in _L0_ffn_all.items() if k in ('Wq_pk', 'pk_keys', 'Wq', 'keys_table', 'values_table', 'Wo')}
    del _L0_ffn_all
    return {'x': x, 'x_txt': x_txt, 'L0_tok_W': _L0_tok_in['W'], 'L0_tok_b': _L0_tok_in['b'], 'L0_txt_emb': _L0_txt_in['emb'], 'L0_txt_W_upd': _L0_txt_in['W_upd'], 'L0_txt_b_upd': _L0_txt_in['b_upd'], 'L0_txt_W_f': _L0_txt_in['W_f'], 'L0_txt_b_f': _L0_txt_in['b_f'], 'L0_txt_decay_param': _L0_txt_in['decay_param'], 'L0_txt_norm_g': _L0_txt_in['norm_g'], 'L0_txt_norm_b': _L0_txt_in['norm_b'], 'L0_txt_cms_ln_g': _L0_txt_in['cms_ln_g'], 'L0_txt_cms_ln_b': _L0_txt_in['cms_ln_b'], 'L0_txt_cms_W1': _L0_txt_in['cms_W1'], 'L0_txt_cms_b1': _L0_txt_in['cms_b1'], 'L0_txt_cms_W2': _L0_txt_in['cms_W2'], 'L0_txt_cms_b2': _L0_txt_in['cms_b2'], 'L0_txt_head_W': _L0_txt_in['head_W'], 'L0_txt_head_b': _L0_txt_in['head_b'], 'L0_attn_fw_W_in': _L0_attn_in['fw_W_in'], 'L0_attn_fw_conv_w': _L0_attn_in['fw_conv_w'], 'L0_attn_fw_conv_b': _L0_attn_in['fw_conv_b'], 'L0_attn_fw_W_x': _L0_attn_in['fw_W_x'], 'L0_attn_fw_W_dt': _L0_attn_in['fw_W_dt'], 'L0_attn_fw_b_dt': _L0_attn_in['fw_b_dt'], 'L0_attn_fw_A_log': _L0_attn_in['fw_A_log'], 'L0_attn_fw_D': _L0_attn_in['fw_D'], 'L0_attn_fw_W_out': _L0_attn_in['fw_W_out'], 'L0_attn_bw_W_in': _L0_attn_in['bw_W_in'], 'L0_attn_bw_conv_w': _L0_attn_in['bw_conv_w'], 'L0_attn_bw_conv_b': _L0_attn_in['bw_conv_b'], 'L0_attn_bw_W_x': _L0_attn_in['bw_W_x'], 'L0_attn_bw_W_dt': _L0_attn_in['bw_W_dt'], 'L0_attn_bw_b_dt': _L0_attn_in['bw_b_dt'], 'L0_attn_bw_A_log': _L0_attn_in['bw_A_log'], 'L0_attn_bw_D': _L0_attn_in['bw_D'], 'L0_attn_bw_W_out': _L0_attn_in['bw_W_out'], 'L0_attn_merge_W': _L0_attn_in['merge_W'], 'L0_ffn_Wq_pk': _L0_ffn_in['Wq_pk'], 'L0_ffn_pk_keys': _L0_ffn_in['pk_keys'], 'L0_ffn_Wq': _L0_ffn_in['Wq'], 'L0_ffn_keys_table': _L0_ffn_in['keys_table'], 'L0_ffn_values_table': _L0_ffn_in['values_table'], 'L0_ffn_Wo': _L0_ffn_in['Wo']}

def reference(x, x_txt, L0_tok_W, L0_tok_b, L0_txt_emb, L0_txt_W_upd, L0_txt_b_upd, L0_txt_W_f, L0_txt_b_f, L0_txt_decay_param, L0_txt_norm_g, L0_txt_norm_b, L0_txt_cms_ln_g, L0_txt_cms_ln_b, L0_txt_cms_W1, L0_txt_cms_b1, L0_txt_cms_W2, L0_txt_cms_b2, L0_txt_head_W, L0_txt_head_b, L0_attn_fw_W_in, L0_attn_fw_conv_w, L0_attn_fw_conv_b, L0_attn_fw_W_x, L0_attn_fw_W_dt, L0_attn_fw_b_dt, L0_attn_fw_A_log, L0_attn_fw_D, L0_attn_fw_W_out, L0_attn_bw_W_in, L0_attn_bw_conv_w, L0_attn_bw_conv_b, L0_attn_bw_W_x, L0_attn_bw_W_dt, L0_attn_bw_b_dt, L0_attn_bw_A_log, L0_attn_bw_D, L0_attn_bw_W_out, L0_attn_merge_W, L0_ffn_Wq_pk, L0_ffn_pk_keys, L0_ffn_Wq, L0_ffn_keys_table, L0_ffn_values_table, L0_ffn_Wo):
    import jax
    import jax.numpy as jnp

    def _L0_tok_ref(x, W, b):
        import jax, jax.numpy as jnp
        import numpy as np
        IMAGE_SIZE = 64
        PATCH = 16
        EMBED_DIM = 64
        IN_CH = 3
        BATCH = 128
        IN_DIM = IN_CH * PATCH * PATCH

        def _patchify(x, p):
            B, C, H, Wd = x.shape
            x = x.reshape(B, C, H // p, p, Wd // p, p)
            x = x.transpose(0, 2, 4, 1, 3, 5)
            return x.reshape(B, H // p * (Wd // p), C * p * p)
        patches = _patchify(x, PATCH)
        return jnp.einsum('bnk,ek->bne', patches, W) + b

    def _L0_txt_ref(tokens, emb, W_upd, b_upd, W_f, b_f, decay_param, norm_g, norm_b, cms_ln_g, cms_ln_b, cms_W1, cms_b1, cms_W2, cms_b2, head_W, head_b):
        import jax, jax.numpy as jnp
        import numpy as np
        D_MODEL = 128
        N_LAYERS = 4
        VOCAB = 64
        SEQ = 512
        BATCH = 8
        EPS = 1e-05

        def _ln(x, g, b):
            mu = jnp.mean(x, axis=-1, keepdims=True)
            var = jnp.mean(jnp.square(x - mu), axis=-1, keepdims=True)
            return (x - mu) * jax.lax.rsqrt(var + EPS) * g + b

        def _fast_memory(x, mask, W_upd, b_upd, W_f, b_f, decay_param):
            decay = jax.nn.sigmoid(decay_param[0])
            u = jnp.einsum('bsd,de->bse', x, W_upd) + b_upd
            u_t = jnp.swapaxes(u, 0, 1)
            m_t = jnp.swapaxes(mask, 0, 1)[..., None]

            def step(mem, inp):
                u_i, msk = inp
                new = decay * mem + u_i
                mem = msk * new + (1.0 - msk) * mem
                return (mem, mem)
            mem0 = jnp.zeros((x.shape[0], x.shape[2]), x.dtype)
            _, mems = jax.lax.scan(step, mem0, (u_t, m_t))
            mems = jnp.swapaxes(mems, 0, 1)
            return jnp.einsum('bsd,de->bse', mems, W_f) + b_f
        mask = (tokens != 0).astype(emb.dtype)
        x = emb[tokens]
        x = x + _fast_memory(x, mask, W_upd, b_upd, W_f, b_f, decay_param)
        x = _ln(x, norm_g, norm_b)
        for i in range(N_LAYERS):
            h = _ln(x, cms_ln_g[i], cms_ln_b[i])
            h = jax.nn.gelu(jnp.einsum('bsd,df->bsf', h, cms_W1[i]) + cms_b1[i], approximate=False)
            h = jnp.einsum('bsf,fd->bsd', h, cms_W2[i]) + cms_b2[i]
            x = x + h
        return jnp.einsum('bsd,dv->bsv', x, head_W) + head_b

    def _L0_attn_ref(x, fw_W_in, fw_conv_w, fw_conv_b, fw_W_x, fw_W_dt, fw_b_dt, fw_A_log, fw_D, fw_W_out, bw_W_in, bw_conv_w, bw_conv_b, bw_W_x, bw_W_dt, bw_b_dt, bw_A_log, bw_D, bw_W_out, merge_W):
        import jax, jax.numpy as jnp
        from jax import lax
        import numpy as np
        D_MODEL = 64
        D_INNER = 128
        D_STATE = 16
        D_CONV = 4
        DT_RANK = 16
        B = 2
        T = 1024

        def _mamba(x, W_in, conv_w, conv_b, W_x, W_dt, b_dt, A_log, D, W_out):
            b, t, _ = x.shape
            xz = x @ W_in
            xi, z = jnp.split(xz, 2, axis=-1)
            xc = lax.conv_general_dilated(xi.transpose(0, 2, 1), conv_w[:, None, :], (1,), [(D_CONV - 1, 0)], dimension_numbers=('NCH', 'OIH', 'NCH'), feature_group_count=D_INNER)
            xi = jax.nn.silu(xc.transpose(0, 2, 1) + conv_b)
            xdbl = xi @ W_x
            dt, Bm, Cm = jnp.split(xdbl, [DT_RANK, DT_RANK + D_STATE], axis=-1)
            dt = jax.nn.softplus(dt @ W_dt + b_dt)
            A = -jnp.exp(A_log)
            dA = jnp.exp(dt[..., None] * A)
            dBx = dt[..., None] * Bm[:, :, None, :] * xi[..., None]

            def step(h, ins):
                dA_t, dBx_t, C_t = ins
                h = dA_t * h + dBx_t
                y = jnp.einsum('bdn,bn->bd', h, C_t)
                return (h, y)
            h0 = jnp.zeros((b, D_INNER, D_STATE), x.dtype)
            _, ys = lax.scan(step, h0, (dA.transpose(1, 0, 2, 3), dBx.transpose(1, 0, 2, 3), Cm.transpose(1, 0, 2)))
            y = ys.transpose(1, 0, 2) + xi * D
            y = y * jax.nn.silu(z)
            return y @ W_out

        def _mamba_params(key, prefix):
            ks = jax.random.split(key, 6)
            s = 0.02
            return {prefix + '_W_in': jax.random.normal(ks[0], (D_MODEL, 2 * D_INNER)) * s, prefix + '_conv_w': jax.random.normal(ks[1], (D_INNER, D_CONV)) * s, prefix + '_conv_b': jnp.zeros((D_INNER,), jnp.float32), prefix + '_W_x': jax.random.normal(ks[2], (D_INNER, DT_RANK + 2 * D_STATE)) * s, prefix + '_W_dt': jax.random.normal(ks[3], (DT_RANK, D_INNER)) * s, prefix + '_b_dt': jax.random.normal(ks[4], (D_INNER,)) * s, prefix + '_A_log': jnp.log(jnp.tile(jnp.arange(1, D_STATE + 1, dtype=jnp.float32), (D_INNER, 1))), prefix + '_D': jnp.ones((D_INNER,), jnp.float32), prefix + '_W_out': jax.random.normal(ks[5], (D_INNER, D_MODEL)) * s}
        out_f = _mamba(x, fw_W_in, fw_conv_w, fw_conv_b, fw_W_x, fw_W_dt, fw_b_dt, fw_A_log, fw_D, fw_W_out)
        out_b = jnp.flip(_mamba(jnp.flip(x, 1), bw_W_in, bw_conv_w, bw_conv_b, bw_W_x, bw_W_dt, bw_b_dt, bw_A_log, bw_D, bw_W_out), 1)
        return jnp.concatenate([out_f, out_b], axis=-1) @ merge_W

    def _L0_ffn_ref(x, Wq_pk, pk_keys, Wq, keys_table, values_table, Wo):
        import jax, jax.numpy as jnp
        import numpy as np
        DIM = 64
        HEADS = 8
        NUM_KEYS = 64
        NUM_KV = NUM_KEYS ** 2
        PK_TOPK = 16
        FINAL_TOPK = 16
        DIM_KEY = DIM // 2
        P = 2

        def _pk(x, Wq_pk, pk_keys):
            b, n, _ = x.shape
            q = (x @ Wq_pk).reshape(b, n, P, HEADS, DIM_KEY).transpose(2, 0, 1, 3, 4)
            sim = jnp.einsum('pbnhd,pkhd->pbnhk', q, pk_keys)
            scores, idx = jax.lax.top_k(sim, PK_TOPK)
            idx0 = idx[0]
            idx1 = idx[1] * NUM_KEYS
            index = (idx0[..., :, None] + idx1[..., None, :]).reshape(b, n, HEADS, PK_TOPK * PK_TOPK)
            score = (scores[0][..., :, None] + scores[1][..., None, :]).reshape(b, n, HEADS, PK_TOPK * PK_TOPK)
            final_scores, pk_idx = jax.lax.top_k(score, FINAL_TOPK)
            final_indices = jnp.take_along_axis(index, pk_idx, axis=-1)
            final_scores = jax.nn.softmax(final_scores, axis=-1)
            return (final_scores, final_indices)
        b, n, d = x.shape
        q = (x @ Wq).reshape(b, n, HEADS, DIM) * DIM ** (-0.5)
        kv_scores, indices = _pk(x, Wq_pk, pk_keys)
        offsets = jnp.arange(HEADS, dtype=indices.dtype) * NUM_KV
        ind = indices + offsets[None, None, :, None]
        k = jnp.einsum('bnhk,bnhkd->bnhd', kv_scores, keys_table[ind])
        v = jnp.einsum('bnhk,bnhkd->bnhd', kv_scores, values_table[ind])
        sim = jnp.einsum('bihd,bjhd->bhij', q, k)
        neg = -jnp.finfo(sim.dtype).max
        causal = jnp.tril(jnp.ones((n, n), dtype=bool))
        sim = jnp.where(causal, sim, neg)
        attn = jax.nn.softmax(sim, axis=-1)
        out = jnp.einsum('bhij,bjhd->bhid', attn, v)
        out = out.transpose(0, 2, 1, 3).reshape(b, n, HEADS * DIM)
        return out @ Wo
    h = _L0_tok_ref(x, L0_tok_W, L0_tok_b)
    h = jnp.concatenate([h, _L0_txt_ref(x_txt, L0_txt_emb, L0_txt_W_upd, L0_txt_b_upd, L0_txt_W_f, L0_txt_b_f, L0_txt_decay_param, L0_txt_norm_g, L0_txt_norm_b, L0_txt_cms_ln_g, L0_txt_cms_ln_b, L0_txt_cms_W1, L0_txt_cms_b1, L0_txt_cms_W2, L0_txt_cms_b2, L0_txt_head_W, L0_txt_head_b)], axis=1)
    h = h + _L0_attn_ref(_layernorm(h, axis=-1), L0_attn_fw_W_in, L0_attn_fw_conv_w, L0_attn_fw_conv_b, L0_attn_fw_W_x, L0_attn_fw_W_dt, L0_attn_fw_b_dt, L0_attn_fw_A_log, L0_attn_fw_D, L0_attn_fw_W_out, L0_attn_bw_W_in, L0_attn_bw_conv_w, L0_attn_bw_conv_b, L0_attn_bw_W_x, L0_attn_bw_W_dt, L0_attn_bw_b_dt, L0_attn_bw_A_log, L0_attn_bw_D, L0_attn_bw_W_out, L0_attn_merge_W)
    h = h + _L0_ffn_ref(_layernorm(h, axis=-1), L0_ffn_Wq_pk, L0_ffn_pk_keys, L0_ffn_Wq, L0_ffn_keys_table, L0_ffn_values_table, L0_ffn_Wo)
    return h

_drawn_inputs = setup_inputs


def setup_inputs(seed=0):
    import zlib

    import numpy as np

    out = dict(_drawn_inputs(seed))
    spreads = {'L0_txt_b_upd': (0.0, 0.1),
     'L0_txt_b_f': (0.0, 0.1),
     'L0_txt_norm_g': (1.0, 0.2),
     'L0_txt_norm_b': (0.0, 0.1),
     'L0_txt_cms_ln_g': (1.0, 0.6),
     'L0_txt_cms_ln_b': (0.0, 0.8),
     'L0_txt_cms_b1': (0.0, 0.525),
     'L0_txt_cms_b2': (0.0, 0.1),
     'L0_txt_head_b': (0.0, 0.1),
     'L0_attn_fw_conv_b': (0.0, 0.8),
     'L0_attn_fw_D': (1.0, 0.6),
     'L0_attn_bw_conv_b': (0.0, 0.8),
     'L0_attn_bw_D': (1.0, 0.6)}
    factors = {'L0_tok_b': 17.324,
     'L0_txt_W_upd': 8.0,
     'L0_attn_fw_W_in': 8.0,
     'L0_attn_fw_conv_w': 8.0,
     'L0_attn_fw_W_x': 8.0,
     'L0_attn_fw_W_dt': 8.0,
     'L0_attn_fw_b_dt': 8.0,
     'L0_attn_fw_A_log': 8.0,
     'L0_attn_fw_W_out': 8.0,
     'L0_attn_bw_W_in': 8.0,
     'L0_attn_bw_conv_w': 8.0,
     'L0_attn_bw_W_x': 8.0,
     'L0_attn_bw_W_dt': 8.0,
     'L0_attn_bw_b_dt': 8.0,
     'L0_attn_bw_A_log': 43.946,
     'L0_attn_bw_W_out': 8.0,
     'L0_attn_merge_W': 8.0,
     'L0_ffn_Wq_pk': 64.0,
     'L0_ffn_pk_keys': 64.0,
     'L0_ffn_Wq': 64.0,
     'L0_ffn_keys_table': 64.0,
     'L0_ffn_values_table': 64.0,
     'L0_ffn_Wo': 64.0}
    for name, (base, spread) in spreads.items():
        noise = np.random.default_rng([zlib.crc32(name.encode()), seed]).standard_normal(out[name].shape)
        drawn = base * np.exp(spread * noise) if base else spread * noise
        out[name] = jnp.asarray(drawn.astype(out[name].dtype))
    for name, factor in factors.items():
        out[name] = (out[name] * factor).astype(out[name].dtype)
    return out
```

```python
from contextlib import ExitStack

import numpy as np

import concourse.bass as bass
from concourse import mybir

ALU = mybir.AluOpType
ACT = mybir.ActivationFunctionType
AX = mybir.AxisListType
F32 = mybir.dt.float32
I32 = mybir.dt.int32
U32 = mybir.dt.uint32

B = 64
NI, NT = 36, 77
T = NI + NT
KC = 6
E = 64
DM = 128
VOCAB = 64
LAYERS = 4
FC = 4
NS = 16
RK = 16
TAPS = 4
NG = 4
H = 8
NK = 64
TOP = 16
KV = 2 * E
CA, CB = 4 * TOP, 12 * 4
CAND = CA + CB
LOWEST = -3.0e38
EPS = 1e-5
SPLIT = 6
LOG_EXP = "natural_log_exp_and_others"
LOG_MAX = 87.0
CAP_LOG_MAX = 83.0
DECAY_END = 104.0

COLS = ['b_upd', 'b_f', 'norm_g', 'norm_b', 'decay', 'eps', 'iota']
WIDE = [('ident', DM), ('mean128', DM), ('w_upd', DM), ('w_f', DM),
        ('w1', LAYERS * FC * DM), ('w2', LAYERS * FC * DM), ('head_w', E), ('tok_w', KC * E),
        ('ln_g', LAYERS), ('ln_b', LAYERS), ('b1', LAYERS * FC), ('b2', LAYERS),
        ('w_x', 2 * (RK + 2 * NS)), ('w_out', 2 * E), ('conv_w', 2 * TAPS), ('conv_b', 2), ('b_dt', 2),
        ('a_log', 2 * NS), ('skip_d', 2), ('pk_keys', 4 * 4 * NK), ('causal', T), ('iota16', TOP),
        ('head_base', H * TOP)] + [(c, 1) for c in COLS]
SLIM = [('emb', DM), ('mean64', E), ('w_in', 2 * 2 * DM), ('w_dt', 2 * DM), ('merge', 2 * E),
        ('wq_pk', 4 * DM), ('wq', H * E), ('wo', H * E), ('tok_b', 1), ('head_b', 1)]


def offsets(parts):
    at, out = 0, {}
    for name, n in parts:
        out[name] = (at, n)
        at += n
    return out, at


WIDE_AT, WIDE_N = offsets(WIDE)
SLIM_AT, SLIM_N = offsets(SLIM)


class Signal:

    def __init__(self, sem, steps):
        self.sem, self.steps, self.next = sem, steps, 0

    def at(self, b, step):
        return self.sem, b * len(self.steps) + self.steps.index(step) + 1

    def of(self, step):
        assert self.steps[self.next] == step, (self.steps[self.next], step)
        self.next = (self.next + 1) % len(self.steps)
        return self.sem, 1


class LoopTurn:

    def __init__(self, value, parity):
        self.value, self.parity = value, parity


TURN = """M M T M T H M h M H h A T M M M T M T T M A L T A L M A A L L M T M M T M K K L l l T l K K K K K T
          K K T l K l K L T K T T l T K T K"""


def idle(steps):
    for _ in range(steps):
        yield


def each(*names):
    return [f"{n}{i}" for i in range(LAYERS) for n in names]


def fused_embed_kernel(nc, x, tokens, wide_d, slim_d, table, out):
    with ExitStack() as ctx:
        def sb(name, shape, dt=F32):
            return ctx.enter_context(nc.sbuf_tensor(name, shape, dt))

        def bank(name):
            return ctx.enter_context(nc.psum_tensor(name, [128, 512], F32))

        def signal(name, steps):
            return Signal(ctx.enter_context(nc.semaphore(name)), steps)

        def sem(name):
            return ctx.enter_context(nc.semaphore(name))

        wide = sb("wide", [128, WIDE_N])
        slim = sb("slim", [64, SLIM_N])

        def W(name):
            a, n = WIDE_AT[name]
            return wide[:, a:a + n]

        def S(name):
            a, n = SLIM_AT[name]
            return slim[:, a:a + n]

        def col(name, i=0):
            a, _ = WIDE_AT[name]
            return wide[:, a + i:a + i + 1]

        def scol(name):
            a, _ = SLIM_AT[name]
            return slim[:, a:a + 1]

        ident = W('ident')
        w1 = W('w1').rearrange("p (l c f) -> p l c f", l=LAYERS, c=FC)
        w2 = W('w2').rearrange("p (l c f) -> p l c f", l=LAYERS, c=FC)
        tok_w = W('tok_w').rearrange("p (c e) -> p c e", c=KC)
        w_x = W('w_x').rearrange("p (r n) -> p r n", r=2)
        w_out = W('w_out').rearrange("p (r n) -> p r n", r=2)
        w_in = S('w_in').rearrange("p (r z n) -> p r z n", r=2, z=2)
        w_dt = S('w_dt')[0:RK, :].rearrange("p (r n) -> p r n", r=2)
        merge = S('merge').rearrange("p (r n) -> p r n", r=2)
        pk_keys = W('pk_keys').rearrange("p (c n) -> p c n", c=4)
        wq_pk = S('wq_pk').rearrange("p (c n) -> p c n", c=4)
        wq = S('wq').rearrange("p (h n) -> p h n", h=H)
        wo = S('wo').rearrange("p (h n) -> p h n", h=H)

        xin = sb("xin", [128, 2, KC, NI])
        tok_i = sb("tok_i", [128, 2, NT], I32)
        tok_f = sb("tok_f", [128, NT])
        onehot = sb("onehot", [64, NT])
        mask = sb("mask", [128, NT])
        keep = sb("keep", [128, NT])
        xe = sb("xe", [128, NT])
        mem_in = sb("mem_in", [128, NT])
        mems = sb("mems", [128, NT])
        xt = sb("xt", [128, NT])
        cen = sb("cen", [128, NT])
        sq = sb("sq", [128, NT])
        lnv = sb("lnv", [128, NT])
        rstd = sb("rstd", [128, NT])
        mcen = sb("mcen", [64, T])
        msq = sb("msq", [64, T])
        mlnv = sb("mlnv", [64, T])
        mrstd = sb("mrstd", [64, T])
        hn = sb("hn", [128, NT])
        hid = sb("hid", [128, FC, NT])
        decay_e = sb("decay_e", [128, 3])
        hT = sb("hT", [64, T])
        nT = sb("nT", [64, 2, T])
        xpad = sb("xpad", [128, 2, TAPS - 1 + T])
        pre = sb("pre", [128, 4, T])
        gate = sb("gate", [128, 4, T])
        act = sb("act", [128, 4, T])
        dtr = sb("dtr", [RK, 2, T])
        dtp = sb("dtp", [128, 2, T])
        dte = sb("dte", [128, 2, T])
        dtl = sb("dtl", [128, 2, T])
        dt = sb("dt", [128, 2, T])
        dtx = sb("dtx", [128, 2, T])
        a_neg = sb("a_neg", [128, 2 * NS])
        dt_cap = sb("dt_cap", [128, 2 * NS])
        decayed = sb("decayed", [128, 2, NS, T])
        state = sb("state", [128, 2, NS, T])
        yv = sb("yv", [128, 2, T])
        oT = sb("oT", [64, 2, T])
        h2T = sb("h2T", [64, 2, T])
        n2T = sb("n2T", [64, T])
        qp = sb("qp", [128, 4, T])
        sims = sb("sims", [T, 2 * H, NK])
        left = sb("left", [T, 2 * H, NK])
        topv = sb("topv", [T, 2, H, TOP])
        topi = sb("topi", [T, 2, H, TOP], U32)
        topf = sb("topf", [T, 2, H, TOP])
        spare = state[:, :, :, :].rearrange("p r n t -> p (r n t)")
        cand = spare[0:T, 0:H * CAND].rearrange("t (h c) -> t h c", h=H)
        cleft = left[:, :, :].rearrange("t g k -> t (g k)")[:, 0:H * CAND].rearrange("t (h c) -> t h c", h=H)
        best = sb("best", [T, H, TOP])
        pos = sb("pos", [T, H, TOP], U32)
        hi_a = sb("hi_a", [T, H * TOP], U32)
        lo_a = sb("lo_a", [T, H * TOP], U32)
        hi_b = sb("hi_b", [T, H * TOP], U32)
        lo_b = sb("lo_b", [T, H * TOP], U32)
        fa = sb("fa", [T, 2, H * TOP])
        fb = sb("fb", [T, 2, H * TOP])
        late = sb("late", [T, H * TOP])
        hit = spare[0:T, H * CAND:H * CAND + H * TOP * TOP].rearrange("t (c r) -> t c r", r=TOP)
        found = sb("found", [T, 2, H * TOP])
        flat = sb("flat", [T, H * TOP])
        rows = sb("rows", [T, 2, H * TOP], I32)
        wraw = sb("wraw", [T, H, TOP])
        wexp = sb("wexp", [T, H, TOP])
        wsum = sb("wsum", [T, H])
        wrec = sb("wrec", [T, H])
        wts = sb("wts", [T, 2, H, TOP])
        qT = sb("qT", [64, 2, H, T])
        G = sb("G", [T, H, TOP, KV])
        kT = sb("kT", [64, H, T])
        kv = sb("kv", [T, H, KV])
        att = sb("att", [T, H, T])
        attT = sb("attT", [T, H, T])
        rmax = sb("rmax", [T, H])
        rsum = sb("rsum", [T, H])
        rrec = sb("rrec", [T, H])
        oh = sb("oh", [64, H, T])
        res = sb("res", [T, 2, E])

        text_bank, hidden_bank = bank("text_bank"), bank("hidden_bank")
        mix_bank, wide_bank = bank("mix_bank"), bank("wide_bank")
        row_bank = [bank(f"row_bank{i}") for i in range(2)]
        head_bank = [bank(f"head_bank{i}") for i in range(2)]

        weights_in = sem("weights_in")
        x_in = [sem(f"x_in{p}") for p in range(2)]
        tok_in = [sem(f"tok_in{p}") for p in range(2)]
        gathered = [sem(f"gathered{h}") for h in range(H)]
        out_sent = [sem(f"out_sent{p}") for p in range(2)]
        setup_v = sem("setup_v")
        setup_a = sem("setup_a")

        text_v = signal("text_v", ["tokens", "onehot", "mask", "keep", "mem_in", "mems", "x", "center", "scaled", "x_n"]
                        + each("center", "scaled", "h", "x"))
        text_a = signal("text_a", ["embed", "square", "log", "rstd"] + each("square", "log", "rstd", "gelu"))
        text_p = signal("text_p", ["embed", "u", "f", "mean", "var"] + each("mean", "var", "hidden", "out")
                        + ["stream"])
        mix_v = signal("mix_v", ["center", "n_fwd", "n_bwd", "conv0", "conv1", "conv2", "conv3", "gate1", "gate2",
                                 "silu", "dt", "dt_a_f", "dt_a_b", "dtx"]
                       + ["b_f0", "b_f1", "b_f2", "b_f3", "scan_f", "b_b0", "b_b1", "b_b2", "b_b3", "scan_b"]
                       + ["c_f0", "c_f1", "c_f2", "c_f3", "c_b0", "c_b1", "c_b2", "c_b3"]
                       + ["y_skip", "y", "h2", "center2", "n2"])
        mix_a = signal("mix_a", ["stream", "square", "log", "rstd", "pad", "z", "gate", "dt_low", "dt_pre", "abs",
                                 "exp", "dt_log", "decay_f", "decay_b", "o", "square2", "log2", "rstd2"])
        mix_p = signal("mix_p", ["mean", "var", "xz", "dt_low", "dt_pre"]
                       + ["b_f0", "b_f1", "b_f2", "b_f3", "b_b0", "b_b1", "b_b2", "b_b3"]
                       + ["c_f0", "c_f1", "c_f2", "c_f3", "c_b0", "c_b1", "c_b2", "c_b3"]
                       + ["y", "o", "merged", "mean2", "var2"])
        key_p = signal("key_p", ["q", "sims", "heads"])
        key_a = signal("key_a", ["q", "sims", "heads", "wexp"])
        key_v = signal("key_v", ["top8", "left", "top16", "index", "index_f", "cand_a", "cand_b", "best8", "cleft",
                                 "best16", "wraw", "pos", "bits", "bits_f", "ranks_a", "ranks_b", "hit0", "pick0", "found0",
                                 "hit1", "pick1", "found1", "flat", "rows", "wsum", "wrec", "wts"])
        sum_v = signal("sum_v", [f"h{h}" for h in range(H)])
        sum_p = signal("sum_p", [f"h{h}" for h in range(H)])
        sum_a = signal("sum_a", [f"h{h}" for h in range(H)])
        att_p = signal("att_p", ["keys", "sim", "turn", "mixed", "out"])
        att_v = signal("att_v", ["masked", "max", "less", "sum", "rec", "probs"])
        att_a = signal("att_a", ["keys", "exp", "turn", "mixed", "out"])

        block = ctx.enter_context(nc.Block())

        def turn(stages, n, i):
            text, mix, keys, weigh_low, weigh_high, sums_low, sums_high, attend = stages
            p = n % 2 if isinstance(n, int) else n.parity
            b = n if isinstance(n, int) else n.value
            last, this, after, next2 = ((b - 1, 1 - p, i - 1 + p), (b, p, i), (b + 1, 1 - p, i + p), (b + 2, p, i + 1))
            running = {}
            if not isinstance(n, int) or n + 2 < B:
                running["T"] = text(*next2)
            if not isinstance(n, int) or -1 <= n < B - 1:
                running["M"], running["K"] = mix(*after), keys(*after)
            if not isinstance(n, int) or 0 <= n < B:
                running["L"], running["l"] = weigh_low(*this), sums_low(*this)
            if not isinstance(n, int) or n >= 1:
                running["H"], running["h"] = weigh_high(*last), sums_high(*last)
                running["A"] = attend(*last)
            for name in TURN.split():
                if name in running:
                    next(running[name])
            for steps in running.values():
                assert next(steps, "done") == "done"

        def schedule(eng, *stages):
            for n in range(-2, 2):
                turn(stages, n, n // 2)
            with eng.Fori(1, B // 2 - 1) as i:
                turn(stages, LoopTurn(i * 2, 0), i)
                turn(stages, LoopTurn(i * 2 + 1, 1), i)
            for n in range(B - 2, B + 1):
                turn(stages, n, n // 2)

        def first(b, n=1):
            return isinstance(b, int) and b < n

        @block.sync
        def _(sp):
            sp.dma_start(wide[:, :], wide_d).then_inc(weights_in, 16)
            sp.dma_start(slim[:, :], slim_d).then_inc(weights_in, 16)
            token_rows = tokens.rearrange("(b o) t -> b o t", o=1)

            def load(b, p):
                sp.dma_start(xin[:, p, :, :], x[b]).then_inc(x_in[p], 16)
                sp.dma_start(tok_i[:, p, :], token_rows[b].to_broadcast([128, NT])).then_inc(tok_in[p], 16)

            load(0, 0)
            load(1, 1)
            with sp.Fori(0, B // 2 - 1) as i:
                for p in range(2):
                    sp.wait_ge(*text_v.at(i * 2 + p, "tokens"))
                    sp.wait_ge(*text_p.at(i * 2 + p, "stream"))
                    load(i * 2 + 2 + p, p)

        @block.gpsimd
        def _(g):
            def gather(b, p):
                g.wait_ge(*key_v.at(b, "rows"))
                for h in range(H):
                    if not first(b):
                        g.wait_ge(*sum_p.at(b - 1, f"h{h}"))
                    g.nop(nofuse=True)
                    for s in range(TOP):
                        c = h * TOP + s
                        g.indirect_dma_start(
                            out=G[:, h, s, :], out_offset=None, in_=table,
                            in_offset=bass.IndirectOffsetOnAxis(ap=rows[:, p, c:c + 1], axis=0)
                        ).then_inc(gathered[h], 16)

            gather(0, 0)
            gather(1, 1)
            with g.Fori(1, B // 2) as i:
                gather(i * 2, 0)
                gather(i * 2 + 1, 1)

        @block.vector
        def _(v):
            v.memset(xpad[:, :, 0:TAPS - 1], 0.0)
            v.memset(decayed[:, :, :, 0:1], 0.0)
            v.wait_ge(weights_in, 32)
            v.tensor_scalar(dt_cap[:, :], W('a_log'), -CAP_LOG_MAX, LOG_MAX, ALU.max, ALU.min)
            v.tensor_scalar(a_neg[:, :], W('a_log'), LOG_MAX, None, ALU.min).then_inc(setup_v, 1)
            v.wait_ge(setup_a, 1)
            v.tensor_scalar(decay_e[:, 1:2], decay_e[:, 0:1], 1.0, None, ALU.add).then_inc(setup_v, 1)
            v.wait_ge(setup_v, 2)
            v.reciprocal(decay_e[:, 2:3], decay_e[:, 1:2]).then_inc(setup_v, 1)
            v.wait_ge(setup_v, 3)
            v.tensor_scalar(decay_e[:, 0:1], decay_e[:, 2:3], -1.0, None, ALU.add).then_inc(setup_v, 1)
            v.tensor_scalar(dt_cap[:, :], dt_cap[:, :], DECAY_END, None, ALU.mult)
            v.tensor_scalar(a_neg[:, :], a_neg[:, :], -1.0, None, ALU.mult).then_inc(setup_v, 1)
            v.wait_ge(setup_v, 5)
            decay_less = decay_e[:, 0:1]

            def text(b, p, k):
                v.wait_ge(tok_in[p], (k + 1) * 16)
                v.tensor_copy(tok_f[:, :], tok_i[:, p, :]).then_inc(*text_v.of("tokens"))
                v.wait_ge(*text_v.at(b, "tokens"))
                if not first(b):
                    v.wait_ge(*text_p.at(b - 1, "embed"))
                v.tensor_scalar(onehot[:, :], tok_f[0:64, :], col('iota')[0:64], None,
                                ALU.is_equal).then_inc(*text_v.of("onehot"))
                v.tensor_scalar(mask[:, :], tok_f[:, :], 0.0, None, ALU.not_equal).then_inc(*text_v.of("mask"))
                v.wait_ge(*text_v.at(b, "mask"))
                v.tensor_scalar(keep[:, :], mask[:, :], decay_less, 1.0, ALU.mult, ALU.add).then_inc(*text_v.of("keep"))
                yield
                v.wait_ge(*text_p.at(b, "u"))
                v.scalar_tensor_tensor(out=mem_in[:, :], in0=text_bank[:, 128:128 + NT], scalar=col('b_upd'),
                                       in1=mask[:, :], op0=ALU.add, op1=ALU.mult).then_inc(*text_v.of("mem_in"))
                v.wait_ge(*text_v.at(b, "mem_in"))
                v.tensor_tensor_scan(mems[:, :], keep[:, :], mem_in[:, :], 0.0, ALU.mult,
                                     ALU.add).then_inc(*text_v.of("mems"))
                yield
                v.wait_ge(*text_p.at(b, "f"))
                v.scalar_tensor_tensor(out=xt[:, :], in0=text_bank[:, 256:256 + NT], scalar=col('b_f'), in1=xe[:, :],
                                       op0=ALU.add, op1=ALU.add).then_inc(*text_v.of("x"))
                yield
                v.wait_ge(*text_p.at(b, "mean"))
                v.tensor_tensor(cen[:, :], xt[:, :], text_bank[:, 0:NT], ALU.subtract).then_inc(*text_v.of("center"))
                yield
                v.wait_ge(*text_a.at(b, "rstd"))
                v.tensor_tensor(hn[:, :], cen[:, :], rstd[:, :], ALU.mult).then_inc(*text_v.of("scaled"))
                v.wait_ge(*text_v.at(b, "scaled"))
                v.tensor_scalar(xt[:, :], hn[:, :], col('norm_g'), col('norm_b'), ALU.mult,
                                ALU.add).then_inc(*text_v.of("x_n"))
                yield
                for i in range(LAYERS):
                    v.wait_ge(*text_p.at(b, f"mean{i}"))
                    v.tensor_tensor(cen[:, :], xt[:, :], text_bank[:, 0:NT],
                                    ALU.subtract).then_inc(*text_v.of(f"center{i}"))
                    yield
                    v.wait_ge(*text_a.at(b, f"rstd{i}"))
                    v.tensor_tensor(sq[:, :], cen[:, :], rstd[:, :], ALU.mult).then_inc(*text_v.of(f"scaled{i}"))
                    v.wait_ge(*text_v.at(b, f"scaled{i}"))
                    v.tensor_scalar(hn[:, :], sq[:, :], col('ln_g', i), col('ln_b', i), ALU.mult,
                                    ALU.add).then_inc(*text_v.of(f"h{i}"))
                    yield
                    v.wait_ge(*text_p.at(b, f"out{i}"))
                    v.scalar_tensor_tensor(out=xt[:, :], in0=text_bank[:, 256:256 + NT], scalar=col('b2', i),
                                           in1=xt[:, :], op0=ALU.add, op1=ALU.add).then_inc(*text_v.of(f"x{i}"))
                    yield

            def mix(b, p, k):
                yield
                v.wait_ge(*mix_p.at(b, "mean"))
                v.tensor_tensor(mcen[:, :], hT[:, :], mix_bank[0:64, 0:T], ALU.subtract).then_inc(*mix_v.of("center"))
                yield
                v.wait_ge(*mix_a.at(b, "rstd"))
                v.tensor_tensor(nT[:, 0, :], mcen[:, :], mrstd[:, :], ALU.mult).then_inc(*mix_v.of("n_fwd"))
                v.tensor_tensor(nT[:, 1, ::-1], mcen[:, :], mrstd[:, :], ALU.mult).then_inc(*mix_v.of("n_bwd"))
                yield
                v.wait_ge(*mix_a.at(b, "pad"))
                for j in range(TAPS):
                    for r in range(2):
                        if j == 0:
                            ins = v.tensor_scalar(pre[:, r, :], xpad[:, r, 0:T], col('conv_w', r * TAPS),
                                                  col('conv_b', r), ALU.mult, ALU.add)
                        else:
                            if r == 0:
                                v.wait_ge(*mix_v.at(b, f"conv{j - 1}"))
                            ins = v.scalar_tensor_tensor(
                                out=pre[:, r, :], in0=xpad[:, r, j:j + T], scalar=col('conv_w', r * TAPS + j),
                                in1=pre[:, r, :], op0=ALU.mult, op1=ALU.add)
                    ins.then_inc(*mix_v.of(f"conv{j}"))
                yield
                v.wait_ge(*mix_a.at(b, "gate"))
                v.tensor_scalar(gate[:, :, :], gate[:, :, :], 1.0, None, ALU.add).then_inc(*mix_v.of("gate1"))
                v.wait_ge(*mix_v.at(b, "gate1"))
                v.reciprocal(gate[:, :, :], gate[:, :, :]).then_inc(*mix_v.of("gate2"))
                v.wait_ge(*mix_v.at(b, "gate2"))
                v.tensor_tensor(act[:, :, :], pre[:, :, :], gate[:, :, :], ALU.mult).then_inc(*mix_v.of("silu"))
                yield
                v.wait_ge(*mix_a.at(b, "dt_log"))
                v.scalar_tensor_tensor(out=dt[:, :, :], in0=dtp[:, :, :], scalar=0.0, in1=dtl[:, :, :], op0=ALU.max,
                                       op1=ALU.add).then_inc(*mix_v.of("dt"))
                v.wait_ge(*mix_v.at(b, "dt"))
                for r, d in enumerate("fb"):
                    for n in range(NS):
                        c = r * NS + n
                        ins = v.tensor_scalar(decayed[:, r, n, 1:T], dt[:, r, 1:T], dt_cap[:, c:c + 1],
                                              a_neg[:, c:c + 1], ALU.min, ALU.mult)
                    ins.then_inc(*mix_v.of(f"dt_a_{d}"))
                v.tensor_tensor(dtx[:, :, :], dt[:, :, :], act[:, 0:2, :], ALU.mult).then_inc(*mix_v.of("dtx"))
                yield
                v.wait_ge(*mix_v.at(b, "dtx"))
                for r, d in enumerate("fb"):
                    for g in range(NS // NG):
                        v.wait_ge(*mix_p.at(b, f"b_{d}{g}"))
                        bb = row_bank[g % 2][:, 0:NG * T].rearrange("p (n t) -> p n t", n=NG)
                        v.tensor_tensor(state[:, r, g * NG:(g + 1) * NG, :],
                                        dtx[:, r:r + 1, :].to_broadcast([128, NG, T]), bb,
                                        ALU.mult).then_inc(*mix_v.of(f"b_{d}{g}"))
                    v.wait_ge(*mix_a.at(b, f"decay_{d}"))
                    v.wait_ge(*mix_v.at(b, f"b_{d}{NS // NG - 1}"))
                    h_ap = state[:, r, :, :].rearrange("p n t -> p (n t)")
                    v.tensor_tensor_scan(h_ap, decayed[:, r, :, :].rearrange("p n t -> p (n t)"), h_ap, 0.0,
                                         ALU.mult, ALU.add).then_inc(*mix_v.of(f"scan_{d}"))
                    yield
                for r, d in enumerate("fb"):
                    v.wait_ge(*mix_v.at(b, f"scan_{d}"))
                    for g in range(NS // NG):
                        v.wait_ge(*mix_p.at(b, f"c_{d}{g}"))
                        cb = row_bank[g % 2][:, 0:NG * T].rearrange("p (n t) -> p n t", n=NG)
                        hg = state[:, r, g * NG:(g + 1) * NG, :]
                        v.tensor_tensor(hg, hg, cb, ALU.mult).then_inc(*mix_v.of(f"c_{d}{g}"))
                    yield
                v.wait_ge(*mix_p.at(b, "y"))
                for r in range(2):
                    ins = v.scalar_tensor_tensor(out=yv[:, r, :], in0=act[:, r, :], scalar=col('skip_d', r),
                                                 in1=wide_bank[:, r * T:(r + 1) * T], op0=ALU.mult, op1=ALU.add)
                ins.then_inc(*mix_v.of("y_skip"))
                v.wait_ge(*mix_v.at(b, "y_skip"))
                v.tensor_tensor(yv[:, :, :], yv[:, :, :], act[:, 2:4, :], ALU.mult).then_inc(*mix_v.of("y"))
                yield
                v.wait_ge(*mix_p.at(b, "merged"))
                if not first(b, 2):
                    v.wait_ge(*att_p.at(b - 2, "out"))
                v.tensor_tensor(h2T[:, p, :], hT[:, :], mix_bank[0:64, 256:256 + T], ALU.add).then_inc(*mix_v.of("h2"))
                yield
                v.wait_ge(*mix_p.at(b, "mean2"))
                v.tensor_tensor(mcen[:, :], h2T[:, p, :], mix_bank[0:64, 0:T],
                                ALU.subtract).then_inc(*mix_v.of("center2"))
                yield
                v.wait_ge(*mix_a.at(b, "rstd2"))
                v.tensor_tensor(n2T[:, :], mcen[:, :], mrstd[:, :], ALU.mult).then_inc(*mix_v.of("n2"))
                yield
                yield

            def keys(b, p, k):
                groups = [(q, h) for q in range(2) for h in range(H)]
                v.wait_ge(*key_a.at(b, "sims"))
                v.nop(nofuse=True)
                for q, h in groups:
                    ins = v.max(topv[:, q, h, 0:8], sims[:, q * H + h, :])
                ins.then_inc(*key_v.of("top8"))
                yield
                v.wait_ge(*key_v.at(b, "top8"))
                v.nop(nofuse=True)
                for q, h in groups:
                    ins = v.match_replace(left[:, q * H + h, :], topv[:, q, h, 0:8], sims[:, q * H + h, :], LOWEST)
                ins.then_inc(*key_v.of("left"))
                yield
                v.wait_ge(*key_v.at(b, "left"))
                v.nop(nofuse=True)
                for q, h in groups:
                    ins = v.max(topv[:, q, h, 8:16], left[:, q * H + h, :])
                ins.then_inc(*key_v.of("top16"))
                yield
                v.wait_ge(*key_v.at(b, "top16"))
                v.nop(nofuse=True)
                for q, h in groups:
                    v.max_index(topi[:, q, h, 0:8], topv[:, q, h, 0:8], sims[:, q * H + h, :])
                    ins = v.max_index(topi[:, q, h, 8:16], topv[:, q, h, 8:16], left[:, q * H + h, :])
                    if (q, h) == (0, H - 1):
                        yield
                ins.then_inc(*key_v.of("index"))
                yield
                v.wait_ge(*key_v.at(b, "index"))
                v.tensor_copy(topf[:, :, :, :], topi[:, :, :, :]).then_inc(*key_v.of("index_f"))
                v.tensor_tensor(cand[:, :, 0:CA].rearrange("t h (i j) -> t h i j", i=4),
                                topv[:, 0, :, 0:4].unsqueeze(3).to_broadcast([T, H, 4, TOP]),
                                topv[:, 1, :, :].unsqueeze(2).to_broadcast([T, H, 4, TOP]),
                                ALU.add).then_inc(*key_v.of("cand_a"))
                v.tensor_tensor(cand[:, :, CA:CAND].rearrange("t h (i j) -> t h i j", i=12),
                                topv[:, 0, :, 4:16].unsqueeze(3).to_broadcast([T, H, 12, 4]),
                                topv[:, 1, :, 0:4].unsqueeze(2).to_broadcast([T, H, 12, 4]),
                                ALU.add).then_inc(*key_v.of("cand_b"))
                yield
                v.wait_ge(*key_v.at(b, "cand_b"))
                v.nop(nofuse=True)
                for h in range(H):
                    ins = v.max(best[:, h, 0:8], cand[:, h, :])
                ins.then_inc(*key_v.of("best8"))
                yield
                v.wait_ge(*key_v.at(b, "best8"))
                v.nop(nofuse=True)
                for h in range(H):
                    ins = v.match_replace(cleft[:, h, :], best[:, h, 0:8], cand[:, h, :], LOWEST)
                ins.then_inc(*key_v.of("cleft"))
                yield
                v.wait_ge(*key_v.at(b, "cleft"))
                v.nop(nofuse=True)
                for h in range(H):
                    ins = v.max(best[:, h, 8:16], cleft[:, h, :])
                ins.then_inc(*key_v.of("best16"))
                yield
                v.wait_ge(*key_v.at(b, "best16"))
                v.tensor_tensor(wraw[:, :, :], best[:, :, :], best[:, :, 0:1].to_broadcast([T, H, TOP]),
                                ALU.subtract).then_inc(*key_v.of("wraw"))
                for h in range(H):
                    v.max_index(pos[:, h, 0:8], best[:, h, 0:8], cand[:, h, :])
                    ins = v.max_index(pos[:, h, 8:16], best[:, h, 8:16], cleft[:, h, :])
                ins.then_inc(*key_v.of("pos"))
                yield
                v.wait_ge(*key_v.at(b, "pos"))
                pf = pos[:, :, :].rearrange("t h s -> t (h s)")
                v.tensor_scalar(hi_a[:, :], pf, 4, None, ALU.logical_shift_right)
                v.tensor_scalar(lo_a[:, :], pf, 15, None, ALU.bitwise_and)
                v.tensor_scalar(hi_b[:, :], pf, 2, None, ALU.logical_shift_right)
                v.tensor_scalar(lo_b[:, :], pf, 3, None, ALU.bitwise_and)
                v.tensor_scalar(late[:, :], pf, float(CA), None, ALU.is_ge).then_inc(*key_v.of("bits"))
                v.wait_ge(*key_v.at(b, "bits"))
                v.tensor_copy(fa[:, 0, :], hi_a[:, :])
                v.tensor_copy(fa[:, 1, :], lo_a[:, :])
                v.scalar_tensor_tensor(out=fb[:, 0, :], in0=hi_b[:, :], scalar=-12.0, in1=hi_a[:, :], op0=ALU.add,
                                       op1=ALU.subtract)
                v.tensor_tensor(fb[:, 1, :], lo_b[:, :], lo_a[:, :], ALU.subtract).then_inc(*key_v.of("bits_f"))
                v.wait_ge(*key_v.at(b, "bits_f"))
                v.tensor_tensor(fb[:, :, :], fb[:, :, :], late[:, :].unsqueeze(1).to_broadcast([T, 2, H * TOP]),
                                ALU.mult).then_inc(*key_v.of("ranks_a"))
                v.wait_ge(*key_v.at(b, "ranks_a"))
                v.tensor_tensor(fa[:, :, :], fa[:, :, :], fb[:, :, :], ALU.add).then_inc(*key_v.of("ranks_b"))
                yield
                v.wait_ge(*key_v.at(b, "ranks_b"))
                hit4 = hit[:, :, :].rearrange("t (h s) r -> t h s r", h=H)
                for q in range(2):
                    if q == 1:
                        v.wait_ge(*key_v.at(b, "found0"))
                    v.tensor_tensor(hit[:, :, :], fa[:, q, :].unsqueeze(2).to_broadcast([T, H * TOP, TOP]),
                                    W('iota16')[0:T].unsqueeze(1).to_broadcast([T, H * TOP, TOP]),
                                    ALU.is_equal).then_inc(*key_v.of(f"hit{q}"))
                    v.wait_ge(*key_v.at(b, f"hit{q}"))
                    v.tensor_tensor(hit4, hit4, topf[:, q, :, :].unsqueeze(2).to_broadcast([T, H, TOP, TOP]),
                                    ALU.mult).then_inc(*key_v.of(f"pick{q}"))
                    v.wait_ge(*key_v.at(b, f"pick{q}"))
                    v.tensor_reduce(found[:, q, :], hit[:, :, :], AX.X, ALU.add).then_inc(*key_v.of(f"found{q}"))
                    yield
                v.wait_ge(*key_v.at(b, "found1"))
                v.scalar_tensor_tensor(out=flat[:, :], in0=found[:, 1, :], scalar=float(NK), in1=found[:, 0, :],
                                       op0=ALU.mult, op1=ALU.add).then_inc(*key_v.of("flat"))
                v.wait_ge(*key_v.at(b, "flat"))
                if not first(b, 2):
                    v.wait_ge(gathered[H - 1], (b - 1) * 16 * TOP)
                v.tensor_tensor(rows[:, p, :], flat[:, :], W('head_base')[0:T], ALU.add).then_inc(*key_v.of("rows"))
                v.wait_ge(*key_a.at(b, "wexp"))
                v.tensor_reduce(wsum[:, :], wexp[:, :, :], AX.X, ALU.add).then_inc(*key_v.of("wsum"))
                v.wait_ge(*key_v.at(b, "wsum"))
                v.reciprocal(wrec[:, :], wsum[:, :]).then_inc(*key_v.of("wrec"))
                v.wait_ge(*key_v.at(b, "wrec"))
                v.tensor_tensor(wts[:, p, :, :], wexp[:, :, :], wrec[:, :].unsqueeze(2).to_broadcast([T, H, TOP]),
                                ALU.mult).then_inc(*key_v.of("wts"))
                yield

            def weigh(b, p, heads):
                for h in heads:
                    if h == heads[0]:
                        v.wait_ge(*key_v.at(b, "wts"))
                    v.wait_ge(gathered[h], (b + 1) * 16 * TOP)
                    v.tensor_tensor(G[:, h, :, :], G[:, h, :, :],
                                    wts[:, p, h, :].unsqueeze(2).to_broadcast([T, TOP, KV]),
                                    ALU.mult).then_inc(*sum_v.of(f"h{h}"))
                    yield

            def weigh_low(b, p, k):
                return weigh(b, p, range(SPLIT))

            def weigh_high(b, p, k):
                return weigh(b, p, range(SPLIT, H))

            def sums_low(b, p, k):
                return idle(SPLIT)

            def sums_high(b, p, k):
                return idle(H - SPLIT)

            def attend(b, p, k):
                yield
                v.wait_ge(*att_p.at(b, "sim"))
                for c in range(2):
                    ins = v.tensor_tensor(att[:, 4 * c:4 * c + 4, :],
                                          head_bank[c][0:T, 0:4 * T].rearrange("t (h j) -> t h j", h=4),
                                          W('causal')[0:T].unsqueeze(1).to_broadcast([T, 4, T]), ALU.add)
                ins.then_inc(*att_v.of("masked"))
                v.wait_ge(*att_v.at(b, "masked"))
                v.tensor_reduce(rmax[:, :], att[:, :, :], AX.X, ALU.max).then_inc(*att_v.of("max"))
                v.wait_ge(*att_v.at(b, "max"))
                v.tensor_tensor(att[:, :, :], att[:, :, :], rmax[:, :].unsqueeze(2).to_broadcast([T, H, T]),
                                ALU.subtract).then_inc(*att_v.of("less"))
                yield
                v.wait_ge(*att_a.at(b, "exp"))
                v.tensor_reduce(rsum[:, :], att[:, :, :], AX.X, ALU.add).then_inc(*att_v.of("sum"))
                v.wait_ge(*att_v.at(b, "sum"))
                v.reciprocal(rrec[:, :], rsum[:, :]).then_inc(*att_v.of("rec"))
                v.wait_ge(*att_v.at(b, "rec"))
                v.tensor_tensor(att[:, :, :], att[:, :, :], rrec[:, :].unsqueeze(2).to_broadcast([T, H, T]),
                                ALU.mult).then_inc(*att_v.of("probs"))
                yield
                yield
                yield

            schedule(v, text, mix, keys, weigh_low, weigh_high, sums_low, sums_high, attend)

        @block.scalar
        def _(a):
            a.wait_ge(weights_in, 32)
            a.preload_act_table_set(LOG_EXP)
            a.activation(decay_e[:, 0:1], col('decay'), ACT.Exp, scale=-1.0)
            a.wait_ge(setup_v, 1)
            a.activation(a_neg[:, :], a_neg[:, :], ACT.Exp)
            a.activation(dt_cap[:, :], dt_cap[:, :], ACT.Exp, scale=-1.0).then_inc(setup_a, 1)
            a.wait_ge(setup_v, 5)

            def stats(sig, b, cen_ap, sq_ap, lnv_ap, rstd_ap, bank_ap, centre, var_at, names):
                square, log, rstd_name = names
                parts = cen_ap.shape[0]
                a.wait_ge(*centre)
                a.activation(sq_ap, cen_ap, ACT.Square).then_inc(*sig.of(square))
                a.wait_ge(*var_at)
                a.activation(lnv_ap, bank_ap, ACT.Ln, bias=col('eps')[0:parts]).then_inc(*sig.of(log))
                a.wait_ge(*sig.at(b, log))
                a.activation(rstd_ap, lnv_ap, ACT.Exp, scale=-0.5).then_inc(*sig.of(rstd_name))

            def text_stats(b, i):
                stats(text_a, b, cen[:, :], sq[:, :], lnv[:, :], rstd[:, :], text_bank[:, 128:128 + NT],
                      text_v.at(b, f"center{i}"), text_p.at(b, f"var{i}"), (f"square{i}", f"log{i}", f"rstd{i}"))

            def mix_stats(b, i):
                stats(mix_a, b, mcen[:, :], msq[:, :], mlnv[:, :], mrstd[:, :], mix_bank[0:64, 128:128 + T],
                      mix_v.at(b, f"center{i}"), mix_p.at(b, f"var{i}"), (f"square{i}", f"log{i}", f"rstd{i}"))

            def text(b, p, k):
                a.wait_ge(*text_p.at(b, "embed"))
                a.activation(xe[:, :], text_bank[:, 0:NT], ACT.Copy).then_inc(*text_a.of("embed"))
                yield
                yield
                yield
                text_stats(b, "")
                yield
                yield
                for i in range(LAYERS):
                    text_stats(b, i)
                    yield
                    a.wait_ge(*text_p.at(b, f"hidden{i}"))
                    for c in range(FC):
                        ins = a.activation(hid[:, c, :], hidden_bank[:, c * NT:(c + 1) * NT], ACT.Gelu,
                                           bias=col('b1', i * FC + c))
                    ins.then_inc(*text_a.of(f"gelu{i}"))
                    a.preload_act_table_set(LOG_EXP)
                    yield
                    yield

            def mix(b, p, k):
                a.wait_ge(*text_p.at(b, "stream"))
                a.activation(hT[:, 0:NI], hidden_bank[0:64, 384:384 + NI], ACT.Identity, bias=scol('tok_b'))
                a.activation(hT[:, NI:T], hidden_bank[0:64, 384 + NI:384 + T], ACT.Identity,
                             bias=scol('head_b')).then_inc(*mix_a.of("stream"))
                yield
                mix_stats(b, "")
                yield
                a.wait_ge(*mix_p.at(b, "xz"))
                xz = wide_bank[:, 0:4 * T].rearrange("p (c t) -> p c t", c=4)
                a.activation(xpad[:, :, TAPS - 1:], xz[:, 0:2, :], ACT.Copy).then_inc(*mix_a.of("pad"))
                a.activation(pre[:, 2:4, :], xz[:, 2:4, :], ACT.Copy).then_inc(*mix_a.of("z"))
                yield
                a.wait_ge(*mix_a.at(b, "z"))
                a.wait_ge(*mix_v.at(b, "conv3"))
                a.activation(gate[:, :, :], pre[:, :, :], ACT.Exp, scale=-1.0).then_inc(*mix_a.of("gate"))
                yield
                a.wait_ge(*mix_p.at(b, "dt_low"))
                a.activation(dtr[:, :, :], mix_bank[0:RK, 0:2 * T].rearrange("p (r t) -> p r t", r=2),
                             ACT.Copy).then_inc(*mix_a.of("dt_low"))
                a.wait_ge(*mix_p.at(b, "dt_pre"))
                for r in range(2):
                    ins = a.activation(dtp[:, r, :], mix_bank[:, 256 + r * T:256 + (r + 1) * T], ACT.Identity,
                                       bias=col('b_dt', r))
                ins.then_inc(*mix_a.of("dt_pre"))
                a.wait_ge(*mix_a.at(b, "dt_pre"))
                a.activation(dte[:, :, :], dtp[:, :, :], ACT.Abs).then_inc(*mix_a.of("abs"))
                a.wait_ge(*mix_a.at(b, "abs"))
                a.activation(dtl[:, :, :], dte[:, :, :], ACT.Exp, scale=-1.0).then_inc(*mix_a.of("exp"))
                a.wait_ge(*mix_a.at(b, "exp"))
                a.activation(dtl[:, :, :], dtl[:, :, :], ACT.Ln, bias=1.0).then_inc(*mix_a.of("dt_log"))
                yield
                for r, d in enumerate("fb"):
                    a.wait_ge(*mix_v.at(b, f"dt_a_{d}"))
                    a.activation(decayed[:, r, :, 1:T], decayed[:, r, :, 1:T],
                                 ACT.Exp).then_inc(*mix_a.of(f"decay_{d}"))
                yield
                yield
                yield
                yield
                yield
                a.wait_ge(*mix_p.at(b, "o"))
                a.activation(oT[:, 0, :], mix_bank[0:64, 0:T], ACT.Copy)
                a.activation(oT[:, 1, ::-1], mix_bank[0:64, T:2 * T], ACT.Copy).then_inc(*mix_a.of("o"))
                yield
                yield
                mix_stats(b, 2)
                yield
                a.wait_ge(*key_p.at(b, "q"))
                a.activation(qp[:, :, :], wide_bank[:, 0:4 * T].rearrange("p (c t) -> p c t", c=4),
                             ACT.Copy).then_inc(*key_a.of("q"))
                yield
                a.wait_ge(*key_p.at(b, "sims"))
                if not first(b):
                    a.wait_ge(*key_v.at(b - 1, "index"))
                for c in range(2):
                    ins = a.activation(sims[:, c * H:(c + 1) * H, :],
                                       row_bank[c][0:T, :].rearrange("t (h k) -> t h k", h=H), ACT.Copy)
                ins.then_inc(*key_a.of("sims"))
                a.wait_ge(*key_p.at(b, "heads"))
                if not first(b, 2):
                    a.wait_ge(*att_p.at(b - 2, "sim"))
                for c in range(2):
                    ins = a.activation(qT[:, p, 4 * c:4 * c + 4, :],
                                       (mix_bank, wide_bank)[c][0:64, 0:4 * T].rearrange("d (h t) -> d h t", h=4),
                                       ACT.Copy, scale=float(E) ** -0.5)
                ins.then_inc(*key_a.of("heads"))
                yield

            def keys(b, p, k):
                for _ in range(9):
                    yield
                a.wait_ge(*key_v.at(b, "wraw"))
                a.activation(wexp[:, :, :], wraw[:, :, :], ACT.Exp).then_inc(*key_a.of("wexp"))
                for _ in range(5):
                    yield

            def copy_sums(b, heads):
                for h in heads:
                    a.wait_ge(*sum_p.at(b, f"h{h}"))
                    if h == 0 and not first(b):
                        a.wait_ge(*att_p.at(b - 1, "mixed"))
                    a.activation(kv[:, h, :], head_bank[h % 2][0:T, 0:KV], ACT.Copy).then_inc(*sum_a.of(f"h{h}"))
                    yield

            def weigh_low(b, p, k):
                return idle(SPLIT)

            def weigh_high(b, p, k):
                return idle(H - SPLIT)

            def sums_low(b, p, k):
                return copy_sums(b, range(SPLIT))

            def sums_high(b, p, k):
                return copy_sums(b, range(SPLIT, H))

            def attend(b, p, k):
                a.wait_ge(*att_p.at(b, "keys"))
                for c in range(2):
                    ins = a.activation(kT[:, 4 * c:4 * c + 4, :],
                                       head_bank[c][0:64, 0:4 * T].rearrange("d (h t) -> d h t", h=4), ACT.Copy)
                ins.then_inc(*att_a.of("keys"))
                yield
                a.wait_ge(*att_v.at(b, "less"))
                a.activation(att[:, :, :], att[:, :, :], ACT.Exp).then_inc(*att_a.of("exp"))
                yield
                a.wait_ge(*att_p.at(b, "turn"))
                for c in range(2):
                    ins = a.activation(attT[:, 4 * c:4 * c + 4, :],
                                       head_bank[c][0:T, 0:4 * T].rearrange("t (h j) -> t h j", h=4), ACT.Copy)
                ins.then_inc(*att_a.of("turn"))
                yield
                a.wait_ge(*att_p.at(b, "mixed"))
                for c in range(2):
                    ins = a.activation(oh[:, 4 * c:4 * c + 4, :],
                                       head_bank[c][0:64, 0:4 * T].rearrange("d (h t) -> d h t", h=4), ACT.Copy)
                ins.then_inc(*att_a.of("mixed"))
                yield
                a.wait_ge(*att_p.at(b, "out"))
                if not first(b, 2):
                    a.wait_ge(out_sent[p], k * 16)
                a.activation(res[:, p, :], head_bank[0][0:T, 0:E], ACT.Copy).then_inc(*att_a.of("out"))
                a.wait_ge(*att_a.at(b, "out"))
                a.dma_start(out[b], res[:, p, :]).then_inc(out_sent[p], 16)
                yield

            schedule(a, text, mix, keys, weigh_low, weigh_high, sums_low, sums_high, attend)
            for p in range(2):
                a.wait_ge(out_sent[p], 16 * B // 2)

        @block.tensor
        def _(t):
            t.wait_ge(weights_in, 32)

            def mm(o, lhsT, rhs, start=True, stop=True):
                return t.matmul(o, lhsT, rhs, start=start, stop=stop)

            def text(b, p, k):
                t.wait_ge(*text_v.at(b, "onehot"))
                mm(text_bank[:, 0:NT], S('emb'), onehot[:, :]).then_inc(*text_p.of("embed"))
                t.wait_ge(*text_a.at(b, "embed"))
                mm(text_bank[:, 128:128 + NT], W('w_upd'), xe[:, :]).then_inc(*text_p.of("u"))
                yield
                t.wait_ge(*text_v.at(b, "mems"))
                mm(text_bank[:, 256:256 + NT], W('w_f'), mems[:, :]).then_inc(*text_p.of("f"))
                yield

                def mean(i, ready):
                    t.wait_ge(*text_v.at(b, ready))
                    mm(text_bank[:, 0:NT], W('mean128'), xt[:, :]).then_inc(*text_p.of(f"mean{i}"))

                def var(i):
                    t.wait_ge(*text_v.at(b, f"center{i}"))
                    t.wait_ge(*text_a.at(b, f"square{i}"))
                    mm(text_bank[:, 128:128 + NT], W('mean128'), sq[:, :]).then_inc(*text_p.of(f"var{i}"))

                mean("", "x")
                yield
                var("")
                yield
                mean(0, "x_n")
                yield
                for i in range(LAYERS):
                    var(i)
                    yield
                    t.wait_ge(*text_v.at(b, f"h{i}"))
                    if i == 0 and not first(b):
                        t.wait_ge(*mix_a.at(b - 1, "stream"))
                    for c in range(FC):
                        ins = mm(hidden_bank[:, c * NT:(c + 1) * NT], w1[:, i, c, :], hn[:, :])
                    ins.then_inc(*text_p.of(f"hidden{i}"))
                    t.wait_ge(*text_a.at(b, f"gelu{i}"))
                    for c in range(FC):
                        ins = mm(text_bank[:, 256:256 + NT], w2[:, i, c, :], hid[:, c, :], c == 0, c == FC - 1)
                    ins.then_inc(*text_p.of(f"out{i}"))
                    yield
                    if i < LAYERS - 1:
                        mean(i + 1, f"x{i}")
                        yield
                t.wait_ge(x_in[p], (k + 1) * 16)
                for c in range(KC):
                    mm(hidden_bank[0:64, 384:384 + NI], tok_w[:, c, :], xin[:, p, c, :], c == 0, c == KC - 1)
                t.wait_ge(*text_v.at(b, f"x{LAYERS - 1}"))
                mm(hidden_bank[0:64, 384 + NI:384 + T], W('head_w'), xt[:, :]).then_inc(*text_p.of("stream"))
                yield

            def mix(b, p, k):
                def mean(i, x_ap, ready):
                    t.wait_ge(*ready)
                    t.nop(nofuse=True)
                    mm(mix_bank[0:64, 0:T], S('mean64'), x_ap).then_inc(*mix_p.of(f"mean{i}"))

                def var(i):
                    t.wait_ge(*mix_v.at(b, f"center{i}"))
                    t.wait_ge(*mix_a.at(b, f"square{i}"))
                    t.nop(nofuse=True)
                    mm(mix_bank[0:64, 128:128 + T], S('mean64'), msq[:, :]).then_inc(*mix_p.of(f"var{i}"))

                if not first(b):
                    t.wait_ge(*key_a.at(b - 1, "heads"))
                mean("", hT[:, :], mix_a.at(b, "stream"))
                yield
                var("")
                yield
                t.wait_ge(*mix_v.at(b, "n_bwd"))
                for z in range(2):
                    for r in range(2):
                        o = (2 * z + r) * T
                        ins = mm(wide_bank[:, o:o + T], w_in[:, r, z, :], nT[:, r, :])
                ins.then_inc(*mix_p.of("xz"))
                yield
                yield
                t.wait_ge(*mix_v.at(b, "silu"))
                for r in range(2):
                    ins = mm(mix_bank[0:RK, r * T:(r + 1) * T], w_x[:, r, 0:RK], act[:, r, :])
                ins.then_inc(*mix_p.of("dt_low"))
                t.wait_ge(*mix_a.at(b, "dt_low"))
                for r in range(2):
                    ins = mm(mix_bank[:, 256 + r * T:256 + (r + 1) * T], w_dt[:, r, :], dtr[:, r, :])
                ins.then_inc(*mix_p.of("dt_pre"))
                names = [(m, r, g) for m in range(2) for r in range(2) for g in range(NS // NG)]

                def name(c):
                    m, r, g = names[c]
                    return f"{'bc'[m]}_{'fb'[r]}{g}"

                def row_group(c):
                    m, r, g = names[c]
                    if c >= 2:
                        t.wait_ge(*mix_v.at(b, name(c - 2)))
                    for n in range(NG):
                        w = RK + m * NS + g * NG + n
                        ins = mm(row_bank[g % 2][:, n * T:(n + 1) * T],
                                 w_x[:, r, w:w + 1].to_broadcast([128, 128]), act[:, r, :])
                    ins.then_inc(*mix_p.of(name(c)))

                if not first(b):
                    t.wait_ge(*key_a.at(b - 1, "sims"))
                row_group(0)
                row_group(1)
                yield
                yield
                for c in range(2, 6):
                    row_group(c)
                yield
                for c in range(6, 10):
                    row_group(c)
                yield

                def sum_states(r):
                    for n in range(NS):
                        if n % NG == 0:
                            t.wait_ge(*mix_v.at(b, f"c_{'fb'[r]}{n // NG}"))
                        ins = mm(wide_bank[:, r * T:(r + 1) * T], ident, state[:, r, n, :], n == 0, n == NS - 1)
                    return ins

                for c in range(10, 14):
                    row_group(c)
                yield
                row_group(14)
                row_group(15)
                sum_states(0)
                sum_states(1).then_inc(*mix_p.of("y"))
                yield
                t.wait_ge(*mix_v.at(b, "y"))
                for r in range(2):
                    ins = mm(mix_bank[0:64, r * T:(r + 1) * T], w_out[:, r, :], yv[:, r, :])
                ins.then_inc(*mix_p.of("o"))
                t.wait_ge(*mix_a.at(b, "o"))
                t.nop(nofuse=True)
                for r in range(2):
                    ins = mm(mix_bank[0:64, 256:256 + T], merge[:, r, :], oT[:, r, :], r == 0, r == 1)
                ins.then_inc(*mix_p.of("merged"))
                yield
                mean(2, h2T[:, p, :], mix_v.at(b, "h2"))
                yield
                var(2)
                yield
                t.wait_ge(*mix_v.at(b, "n2"))
                for c in range(4):
                    ins = mm(wide_bank[:, c * T:(c + 1) * T], wq_pk[:, c, :], n2T[:, :])
                ins.then_inc(*key_p.of("q"))
                yield
                t.wait_ge(*key_a.at(b, "q"))
                for c in range(4):
                    o = 256 * (c % 2)
                    ins = mm(row_bank[c // 2][0:T, o:o + 256], qp[:, c, :], pk_keys[:, c, :])
                ins.then_inc(*key_p.of("sims"))
                for h in range(H):
                    o = (h % 4) * T
                    ins = mm((mix_bank, wide_bank)[h // 4][0:64, o:o + T], wq[:, h, :], n2T[:, :])
                ins.then_inc(*key_p.of("heads"))
                yield

            def keys(b, p, k):
                for _ in range(14):
                    yield

            def add_rows(b, heads):
                for h in heads:
                    if h == 0 and not first(b):
                        t.wait_ge(*att_a.at(b - 1, "out"))
                    if h >= 2:
                        t.wait_ge(*sum_a.at(b, f"h{h - 2}"))
                    t.wait_ge(*sum_v.at(b, f"h{h}"))
                    for s in range(TOP):
                        ins = mm(head_bank[h % 2][0:T, 0:KV], ident[0:T, 0:T], G[:, h, s, :], s == 0, s == TOP - 1)
                    ins.then_inc(*sum_p.of(f"h{h}"))
                    yield

            def weigh_low(b, p, k):
                return idle(SPLIT)

            def weigh_high(b, p, k):
                return idle(H - SPLIT)

            def sums_low(b, p, k):
                return add_rows(b, range(SPLIT))

            def sums_high(b, p, k):
                return add_rows(b, range(SPLIT, H))

            def attend(b, p, k):
                t.wait_ge(*sum_a.at(b, f"h{H - 1}"))
                t.nop(nofuse=True)
                for h in range(H):
                    o = (h % 4) * T
                    ins = t.transpose(head_bank[h // 4][0:64, o:o + T], kv[:, h, 0:E], ident[0:T, 0:T])
                ins.then_inc(*att_p.of("keys"))
                t.wait_ge(*att_a.at(b, "keys"))
                for h in range(H):
                    o = (h % 4) * T
                    ins = mm(head_bank[h // 4][0:T, o:o + T], qT[:, p, h, :], kT[:, h, :])
                ins.then_inc(*att_p.of("sim"))
                yield
                yield
                t.wait_ge(*att_v.at(b, "probs"))
                for h in range(H):
                    o = (h % 4) * T
                    ins = t.transpose(head_bank[h // 4][0:T, o:o + T], att[:, h, :], ident[0:T, 0:T])
                ins.then_inc(*att_p.of("turn"))
                yield
                t.wait_ge(*att_a.at(b, "turn"))
                for h in range(H):
                    o = (h % 4) * T
                    ins = mm(head_bank[h // 4][0:64, o:o + T], kv[:, h, E:KV], attT[:, h, :])
                ins.then_inc(*att_p.of("mixed"))
                yield
                t.wait_ge(*att_a.at(b, "mixed"))
                t.nop(nofuse=True)
                for h in range(H):
                    mm(head_bank[0][0:T, 0:E], oh[:, h, :], wo[:, h, :], h == 0, False)
                mm(head_bank[0][0:T, 0:E], h2T[:, p, :], ident[0:64, 0:64], False, True).then_inc(*att_p.of("out"))
                yield

            schedule(t, text, mix, keys, weigh_low, weigh_high, sums_low, sums_high, attend)


def kernel(**inputs):
    import concourse.bacc as bacc
    from concourse.bass_utils import run_bass_kernel_spmd

    a = {name: np.asarray(value) for name, value in inputs.items()}

    def txt(name):
        return a['L0_txt_' + name]

    def both(name):
        return np.stack([a[f'L0_attn_{d}_{name}'] for d in ('fw', 'bw')])

    def rows128(w):
        return w.reshape(-1, 128, w.shape[-1]).transpose(1, 0, 2).reshape(128, -1)

    pk = a['L0_ffn_pk_keys']
    blocks = np.zeros((4, 32, 4, 4, NK), np.float32)
    for c in range(4):
        for j in range(4):
            blocks[j, :, c, j, :] = pk[c // 2, :, (c % 2) * 4 + j, :].T
    tri = np.where(np.tril(np.ones((T, T), bool)), 0.0, LOWEST).astype(np.float32)
    causal = np.zeros((128, T), np.float32)
    causal[0:T] = tri
    wide = {
        'ident': np.eye(128, dtype=np.float32), 'mean128': np.full((128, 128), 1.0 / 128, np.float32),
        'w_upd': txt('W_upd'), 'w_f': txt('W_f'),
        'w1': txt('cms_W1').transpose(1, 0, 2).reshape(128, -1),
        'w2': rows128(txt('cms_W2').reshape(-1, 128)),
        'head_w': txt('head_W'), 'tok_w': rows128(a['L0_tok_W'].T),
        'ln_g': txt('cms_ln_g').T, 'ln_b': txt('cms_ln_b').T, 'b1': txt('cms_b1').reshape(-1, 128).T,
        'b2': txt('cms_b2').T, 'w_x': both('W_x').transpose(1, 0, 2).reshape(128, -1),
        'w_out': both('W_out').transpose(1, 0, 2).reshape(128, -1),
        'conv_w': both('conv_w').transpose(1, 0, 2).reshape(128, -1),
        'conv_b': both('conv_b').T, 'b_dt': both('b_dt').T,
        'a_log': both('A_log').transpose(1, 0, 2).reshape(128, -1), 'skip_d': both('D').T,
        'pk_keys': blocks.reshape(128, -1), 'causal': causal,
        'iota16': np.broadcast_to(np.arange(TOP, dtype=np.float32), (128, TOP)),
        'head_base': np.broadcast_to(np.repeat(np.arange(H, dtype=np.float32) * NK * NK, TOP), (128, H * TOP)),
        'b_upd': txt('b_upd')[:, None], 'b_f': txt('b_f')[:, None], 'norm_g': txt('norm_g')[:, None],
        'norm_b': txt('norm_b')[:, None], 'decay': np.broadcast_to(txt('decay_param'), (128, 1)),
        'eps': np.full((128, 1), EPS, np.float32), 'iota': np.arange(128, dtype=np.float32)[:, None],
    }
    w_dt = np.zeros((64, 2 * DM), np.float32)
    w_dt[0:RK] = both('W_dt').transpose(1, 0, 2).reshape(RK, -1)
    slim = {
        'emb': txt('emb'), 'mean64': np.full((64, 64), 1.0 / 64, np.float32),
        'w_in': both('W_in').transpose(1, 0, 2).reshape(64, -1), 'w_dt': w_dt,
        'merge': a['L0_attn_merge_W'].reshape(2, 64, 64).transpose(1, 0, 2).reshape(64, -1),
        'wq_pk': a['L0_ffn_Wq_pk'], 'wq': a['L0_ffn_Wq'],
        'wo': a['L0_ffn_Wo'].reshape(H, 64, 64).transpose(1, 0, 2).reshape(64, -1),
        'tok_b': a['L0_tok_b'][:, None], 'head_b': txt('head_b')[:, None],
    }
    patches = a['x'].reshape(B, 3, 6, 16, 6, 16).transpose(0, 1, 3, 5, 2, 4).reshape(B, KC, 128, NI)
    arrays = {
        'patches': patches.transpose(0, 2, 1, 3), 'tokens': a['x_txt'],
        'wide_w': np.concatenate([wide[n] for n, _ in WIDE], axis=1),
        'slim_w': np.concatenate([slim[n] for n, _ in SLIM], axis=1),
        'table': np.concatenate([a['L0_ffn_keys_table'], a['L0_ffn_values_table']], axis=1),
    }
    arrays = {name: np.ascontiguousarray(value) for name, value in arrays.items()}
    nc = bacc.Bacc("TRN2", target_bir_lowering=False, num_devices=1)
    args = [nc.dram_tensor(name, v.shape, mybir.dt.from_np(v.dtype), kind="ExternalInput").ap()
            for name, v in arrays.items()]
    out = nc.dram_tensor("fused", (B, T, E), F32, kind="ExternalOutput").ap()
    fused_embed_kernel(nc, *args, out)
    r = run_bass_kernel_spmd(nc, [arrays], core_ids=[0])
    return r.results[0]["fused"]
```

```python
from contextlib import ExitStack

import numpy as np

import concourse.bass as bass
from concourse import mybir

ALU = mybir.AluOpType
ACT = mybir.ActivationFunctionType
AX = mybir.AxisListType
F32 = mybir.dt.float32
BF16 = mybir.dt.bfloat16
I32 = mybir.dt.int32
U32 = mybir.dt.uint32

B = 64
NI, NT = 36, 77
T = NI + NT
KC = 6
E = 64
DM = 128
VOCAB = 64
LAYERS = 4
FC = 4
NS = 16
RK = 16
TAPS = 4
NG = 4
H = 8
NK = 64
TOP = 16
KV = 2 * E
CA, CB = 4 * TOP, 12 * 4
CAND = CA + CB
LOWEST = -3.0e38
EPS = 1e-5
PAIRS = H * TOP
BANK_TOKENS = 512 // H
CHUNKS = [16] * 4 + [13, 12, 12, 12]
STARTS = [sum(CHUNKS[:c]) for c in range(len(CHUNKS))]
HALF = STARTS.index(BANK_TOKENS)
BUSY_TOKENS = 16
SPLIT = 6
LOG_EXP = "natural_log_exp_and_others"
LOG_MAX = 87.0
CAP_LOG_MAX = 83.0
DECAY_END = 104.0

COLS = ['b_upd', 'b_f', 'norm_g', 'norm_b', 'decay', 'eps', 'iota']
WIDE = [('ident', DM), ('mean128', DM), ('w_upd', DM), ('w_f', DM),
        ('w1', LAYERS * FC * DM), ('w2', LAYERS * FC * DM), ('head_w', E), ('tok_w', KC * E),
        ('ln_g', LAYERS), ('ln_b', LAYERS), ('b1', LAYERS * FC), ('b2', LAYERS),
        ('w_x', 2 * 128), ('w_out', 2 * E), ('conv_w', 2 * TAPS), ('conv_b', 2), ('b_dt', 2),
        ('a_log', 2 * NS), ('skip_d', 2), ('pk_keys', 4 * 4 * NK), ('causal', T), ('iota16', TOP),
        ('head_base', PAIRS), ('own_head', H), ('own_row', 2 * NS), ('wo', H * E)] + [(c, 1) for c in COLS]
SLIM = [('emb', DM), ('mean64', E), ('w_in', 2 * 2 * DM), ('w_dt', 2 * DM), ('merge', 2 * E),
        ('wq_pk', 4 * DM), ('wq', H * E), ('tok_b', 1), ('head_b', 1)]


def offsets(parts):
    at, out = 0, {}
    for name, n in parts:
        out[name] = (at, n)
        at += n
    return out, at


WIDE_AT, WIDE_N = offsets(WIDE)
SLIM_AT, SLIM_N = offsets(SLIM)


class Signal:

    def __init__(self, sem, steps):
        self.sem, self.steps, self.next = sem, steps, 0

    def at(self, b, step):
        return self.sem, b * len(self.steps) + self.steps.index(step) + 1

    def of(self, step):
        assert self.steps[self.next] == step, (self.steps[self.next], step)
        self.next = (self.next + 1) % len(self.steps)
        return self.sem, 1


class LoopTurn:

    def __init__(self, value, parity):
        self.value, self.parity = value, parity


TURN = """T M T M T T M M H T H T M T M H H M T M A M T A T A M A M M M T T M M L L T K K L K K K K L T L K K
          L K L L K L K T L K T L K K T L K"""


def idle(steps):
    for _ in range(steps):
        yield


def each(*names):
    return [f"{n}{i}" for i in range(LAYERS) for n in names]


def fused_embed_kernel(nc, x, tokens, wide_d, slim_d, table, out):
    with ExitStack() as ctx:
        def sb(name, shape, dt=F32):
            return ctx.enter_context(nc.sbuf_tensor(name, shape, dt))

        def bank(name):
            return ctx.enter_context(nc.psum_tensor(name, [128, 512], F32))

        def signal(name, steps):
            return Signal(ctx.enter_context(nc.semaphore(name)), steps)

        def sem(name):
            return ctx.enter_context(nc.semaphore(name))

        wide = sb("wide", [128, WIDE_N])
        slim = sb("slim", [64, SLIM_N])

        def W(name):
            a, n = WIDE_AT[name]
            return wide[:, a:a + n]

        def S(name):
            a, n = SLIM_AT[name]
            return slim[:, a:a + n]

        def col(name, i=0):
            a, _ = WIDE_AT[name]
            return wide[:, a + i:a + i + 1]

        def scol(name):
            a, _ = SLIM_AT[name]
            return slim[:, a:a + 1]

        ident = W('ident')
        w1 = W('w1').rearrange("p (l c f) -> p l c f", l=LAYERS, c=FC)
        w2 = W('w2').rearrange("p (l c f) -> p l c f", l=LAYERS, c=FC)
        tok_w = W('tok_w').rearrange("p (c e) -> p c e", c=KC)
        w_x = W('w_x').rearrange("p (r n) -> p r n", r=2)
        w_out = W('w_out').rearrange("p (r n) -> p r n", r=2)
        w_in = S('w_in').rearrange("p (r z n) -> p r z n", r=2, z=2)
        w_dt = S('w_dt')[0:RK, :].rearrange("p (r n) -> p r n", r=2)
        merge = S('merge').rearrange("p (r n) -> p r n", r=2)
        pk_keys = W('pk_keys').rearrange("p (c n) -> p c n", c=4)
        wq_pk = S('wq_pk').rearrange("p (c n) -> p c n", c=4)
        wq = S('wq').rearrange("p (h n) -> p h n", h=H)
        wo = W('wo').rearrange("p (h n) -> p h n", h=H)

        xin = sb("xin", [128, 2, KC, NI])
        tok_i = sb("tok_i", [128, 2, NT], I32)
        tok_f = sb("tok_f", [128, NT])
        onehot = sb("onehot", [64, NT])
        mask = sb("mask", [128, NT])
        keep = sb("keep", [128, NT])
        xe = sb("xe", [128, NT])
        mem_in = sb("mem_in", [128, NT])
        mems = sb("mems", [128, NT])
        xt = sb("xt", [128, NT])
        cen = sb("cen", [128, NT])
        sq = sb("sq", [128, NT])
        lnv = sb("lnv", [128, NT])
        rstd = sb("rstd", [128, NT])
        mcen = sb("mcen", [64, T])
        msq = sb("msq", [64, T])
        mlnv = sb("mlnv", [64, T])
        mrstd = sb("mrstd", [64, T])
        hn = sb("hn", [128, NT])
        hid = sb("hid", [128, FC, NT])
        decay_e = sb("decay_e", [128, 3])
        hT = sb("hT", [64, T])
        nT = sb("nT", [64, 2, T])
        xpad = sb("xpad", [128, 2, TAPS - 1 + T])
        pre = sb("pre", [128, 4, T])
        gate = sb("gate", [128, 4, T])
        act = sb("act", [128, 4, T])
        xbc = sb("xbc", [128, 2, T])
        bc_parts = sb("bc_parts", [128, 2, T], BF16)
        own_row = sb("own_row", [128, 2 * NS], BF16)
        dtp = sb("dtp", [128, 2, T])
        dte = sb("dte", [128, 2, T])
        dtl = sb("dtl", [128, 2, T])
        dt = sb("dt", [128, 2, T])
        dtx = sb("dtx", [128, 2, T])
        a_neg = sb("a_neg", [128, 2 * NS])
        dt_cap = sb("dt_cap", [128, 2 * NS])
        decayed = sb("decayed", [128, 2, NS, T])
        state = sb("state", [128, 2, NS, T])
        yv = sb("yv", [128, 2, T])
        oT = sb("oT", [64, 2, T])
        h2T = sb("h2T", [64, 2, T])
        n2T = sb("n2T", [64, T])
        qp = sb("qp", [128, 4, T])
        sims = sb("sims", [T, 2 * H, NK])
        left = sb("left", [T, 2 * H, NK])
        topv = sb("topv", [T, 2, H, TOP])
        topi = sb("topi", [T, 2, H, TOP], U32)
        topf = sb("topf", [T, 2, H, TOP])
        spare = state[:, :, :, :].rearrange("p r n t -> p (r n t)")
        cand = spare[0:T, 0:H * CAND].rearrange("t (h c) -> t h c", h=H)
        cleft = left[:, :, :].rearrange("t g k -> t (g k)")[:, 0:H * CAND].rearrange("t (h c) -> t h c", h=H)
        best = sb("best", [T, H, TOP])
        pos = sb("pos", [T, H, TOP], U32)
        hi_a = sb("hi_a", [T, H * TOP], U32)
        lo_a = sb("lo_a", [T, H * TOP], U32)
        hi_b = sb("hi_b", [T, H * TOP], U32)
        lo_b = sb("lo_b", [T, H * TOP], U32)
        fa = sb("fa", [T, 2, H * TOP])
        fb = sb("fb", [T, 2, H * TOP])
        late = sb("late", [T, H * TOP])
        hit = spare[0:T, H * CAND:H * CAND + H * TOP * TOP].rearrange("t (c r) -> t c r", r=TOP)
        found = sb("found", [T, 2, H * TOP])
        flat = sb("flat", [T, H * TOP])
        rows = sb("rows", [PAIRS, 2, T], I32)
        wraw = sb("wraw", [T, H, TOP])
        wexp = sb("wexp", [T, H, TOP])
        wsum = sb("wsum", [T, H])
        wrec = sb("wrec", [T, H])
        wts = sb("wts", [T, PAIRS])
        spread = sb("spread", [PAIRS, 2, T, H])
        qT = sb("qT", [64, 2, H, T])
        G = sb("G", [PAIRS, T, KV])
        kvT = sb("kvT", [KV, H, T])
        vw = sb("vw", [T, H, E])
        att = sb("att", [T, H, T])
        attT = sb("attT", [T, H, T])
        rmax = sb("rmax", [T, H])
        rsum = sb("rsum", [T, H])
        rrec = sb("rrec", [T, H])
        res = sb("res", [T, 2, E])

        text_bank, hidden_bank = bank("text_bank"), bank("hidden_bank")
        mix_bank, wide_bank = bank("mix_bank"), bank("wide_bank")
        row_bank = [bank(f"row_bank{i}") for i in range(2)]
        head_bank = [bank(f"head_bank{i}") for i in range(2)]

        weights_in = sem("weights_in")
        x_in = [sem(f"x_in{p}") for p in range(2)]
        tok_in = [sem(f"tok_in{p}") for p in range(2)]
        gathered = [sem(f"gathered{c}") for c in range(len(CHUNKS))]
        out_sent = [sem(f"out_sent{p}") for p in range(2)]
        setup_v = sem("setup_v")
        setup_a = sem("setup_a")

        text_v = signal("text_v", ["tokens", "onehot", "mask", "keep", "mem_in", "mems", "x", "center", "scaled", "x_n"]
                        + each("center", "scaled", "h", "x"))
        text_a = signal("text_a", ["embed", "square", "log", "rstd"] + each("square", "log", "rstd", "gelu"))
        text_p = signal("text_p", ["embed", "u", "f", "mean", "var"] + each("mean", "var", "hidden", "out")
                        + ["stream"])
        mix_v = signal("mix_v", ["center", "n_fwd", "n_bwd", "conv0", "conv1", "conv2", "conv3", "gate1", "gate2",
                                 "silu", "bc_hi", "bc_rest", "bc_mid", "bc_last", "bc_lo",
                                 "dt", "dt_a_f", "dt_a_b", "dtx"]
                       + ["b_f0", "b_f1", "b_f2", "b_f3", "scan_f", "b_b0", "b_b1", "b_b2", "b_b3", "scan_b"]
                       + ["c_f0", "c_f1", "c_f2", "c_f3", "c_b0", "c_b1", "c_b2", "c_b3"]
                       + ["y_skip", "y", "h2", "center2", "n2"])
        mix_a = signal("mix_a", ["stream", "square", "log", "rstd", "pad", "z", "gate", "dt_low", "dt_pre", "abs",
                                 "exp", "dt_log", "decay_f", "decay_b", "o", "square2", "log2", "rstd2"])
        mix_p = signal("mix_p", ["mean", "var", "xz", "dt_low", "dt_pre"]
                       + ["b_f0", "b_f1", "b_f2", "b_f3", "b_b0", "b_b1", "b_b2", "b_b3"]
                       + ["c_f0", "c_f1", "c_f2", "c_f3", "c_b0", "c_b1", "c_b2", "c_b3"]
                       + ["y", "o", "merged", "mean2", "var2"])
        key_p = signal("key_p", ["q", "sims", "heads", "rows_turn", "wts_turn"])
        key_a = signal("key_a", ["q", "sims", "heads", "wexp"])
        key_v = signal("key_v", ["top8", "left", "top16", "index", "index_f", "cand_a", "cand_b", "best8", "cleft",
                                 "best16", "wraw", "pos", "bits", "bits_f", "ranks_a", "ranks_b", "hit0", "pick0", "found0",
                                 "hit1", "pick1", "found1", "flat", "rows_f",
                                 "wsum", "wrec", "wts", "rows", "spread"])
        sum_p = signal("sum_p", [f"c{c}" for c in range(len(CHUNKS))])
        sum_a = signal("sum_a", ["low", "high"])
        att_p = signal("att_p", ["sim", "vw", "turn", "out"])
        att_v = signal("att_v", ["masked", "max", "less", "sum", "rec", "probs"])
        att_a = signal("att_a", ["exp", "vw", "turn", "out"])

        block = ctx.enter_context(nc.Block())

        def turn(stages, n, i):
            text, mix, keys, sums_low, sums_high, attend = stages
            p = n % 2 if isinstance(n, int) else n.parity
            b = n if isinstance(n, int) else n.value
            last, this, after, next2 = ((b - 1, 1 - p, i - 1 + p), (b, p, i), (b + 1, 1 - p, i + p), (b + 2, p, i + 1))
            running = {}
            if not isinstance(n, int) or n + 2 < B:
                running["T"] = text(*next2)
            if not isinstance(n, int) or -1 <= n < B - 1:
                running["M"], running["K"] = mix(*after), keys(*after)
            if not isinstance(n, int) or 0 <= n < B:
                running["L"] = sums_low(*this)
            if not isinstance(n, int) or n >= 1:
                running["H"] = sums_high(*last)
                running["A"] = attend(*last)
            for name in TURN.split():
                if name in running:
                    next(running[name])
            for steps in running.values():
                assert next(steps, "done") == "done"

        def schedule(eng, *stages):
            for n in range(-2, 2):
                turn(stages, n, n // 2)
            with eng.Fori(1, B // 2 - 1) as i:
                turn(stages, LoopTurn(i * 2, 0), i)
                turn(stages, LoopTurn(i * 2 + 1, 1), i)
            for n in range(B - 2, B + 1):
                turn(stages, n, n // 2)

        def first(b, n=1):
            return isinstance(b, int) and b < n

        @block.sync
        def _(sp):
            sp.dma_start(wide[:, :], wide_d).then_inc(weights_in, 16)
            sp.dma_start(slim[:, :], slim_d).then_inc(weights_in, 16)
            token_rows = tokens.rearrange("(b o) t -> b o t", o=1)

            def load(b, p):
                sp.dma_start(xin[:, p, :, :], x[b]).then_inc(x_in[p], 16)
                sp.dma_start(tok_i[:, p, :], token_rows[b].to_broadcast([128, NT])).then_inc(tok_in[p], 16)

            load(0, 0)
            load(1, 1)
            with sp.Fori(0, B // 2 - 1) as i:
                for p in range(2):
                    sp.wait_ge(*text_v.at(i * 2 + p, "tokens"))
                    sp.wait_ge(*text_p.at(i * 2 + p, "stream"))
                    load(i * 2 + 2 + p, p)

        @block.gpsimd
        def _(g):
            def gather(b, p):
                g.wait_ge(*key_v.at(b, "rows"))
                for c, n in enumerate(CHUNKS):
                    if not first(b):
                        g.wait_ge(*sum_p.at(b - 1, f"c{c}"))
                    g.nop(nofuse=True)
                    for t in range(STARTS[c], STARTS[c] + n):
                        g.indirect_dma_start(
                            out=G[:, t, :], out_offset=None, in_=table,
                            in_offset=bass.IndirectOffsetOnAxis(ap=rows[:, p, t:t + 1], axis=0)
                        ).then_inc(gathered[c], 16)

            gather(0, 0)
            gather(1, 1)
            with g.Fori(1, B // 2) as i:
                gather(i * 2, 0)
                gather(i * 2 + 1, 1)

        @block.vector
        def _(v):
            v.memset(xpad[:, :, 0:TAPS - 1], 0.0)
            v.memset(decayed[:, :, :, 0:1], 0.0)
            v.wait_ge(weights_in, 32)
            v.tensor_scalar(dt_cap[:, :], W('a_log'), -CAP_LOG_MAX, LOG_MAX, ALU.max, ALU.min)
            v.tensor_scalar(a_neg[:, :], W('a_log'), LOG_MAX, None, ALU.min).then_inc(setup_v, 1)
            v.tensor_copy(own_row[:, :], W('own_row'))
            v.wait_ge(setup_a, 1)
            v.tensor_scalar(decay_e[:, 1:2], decay_e[:, 0:1], 1.0, None, ALU.add).then_inc(setup_v, 1)
            v.wait_ge(setup_v, 2)
            v.reciprocal(decay_e[:, 2:3], decay_e[:, 1:2]).then_inc(setup_v, 1)
            v.wait_ge(setup_v, 3)
            v.tensor_scalar(decay_e[:, 0:1], decay_e[:, 2:3], -1.0, None, ALU.add).then_inc(setup_v, 1)
            v.tensor_scalar(dt_cap[:, :], dt_cap[:, :], DECAY_END, None, ALU.mult)
            v.tensor_scalar(a_neg[:, :], a_neg[:, :], -1.0, None, ALU.mult).then_inc(setup_v, 1)
            v.wait_ge(setup_v, 5)
            decay_less = decay_e[:, 0:1]

            def text(b, p, k):
                v.wait_ge(tok_in[p], (k + 1) * 16)
                v.tensor_copy(tok_f[:, :], tok_i[:, p, :]).then_inc(*text_v.of("tokens"))
                v.wait_ge(*text_v.at(b, "tokens"))
                if not first(b):
                    v.wait_ge(*text_p.at(b - 1, "embed"))
                v.tensor_scalar(onehot[:, :], tok_f[0:64, :], col('iota')[0:64], None,
                                ALU.is_equal).then_inc(*text_v.of("onehot"))
                v.tensor_scalar(mask[:, :], tok_f[:, :], 0.0, None, ALU.not_equal).then_inc(*text_v.of("mask"))
                v.wait_ge(*text_v.at(b, "mask"))
                v.tensor_scalar(keep[:, :], mask[:, :], decay_less, 1.0, ALU.mult, ALU.add).then_inc(*text_v.of("keep"))
                yield
                v.wait_ge(*text_p.at(b, "u"))
                v.scalar_tensor_tensor(out=mem_in[:, :], in0=text_bank[:, 128:128 + NT], scalar=col('b_upd'),
                                       in1=mask[:, :], op0=ALU.add, op1=ALU.mult).then_inc(*text_v.of("mem_in"))
                v.wait_ge(*text_v.at(b, "mem_in"))
                v.tensor_tensor_scan(mems[:, :], keep[:, :], mem_in[:, :], 0.0, ALU.mult,
                                     ALU.add).then_inc(*text_v.of("mems"))
                yield
                v.wait_ge(*text_p.at(b, "f"))
                v.scalar_tensor_tensor(out=xt[:, :], in0=text_bank[:, 256:256 + NT], scalar=col('b_f'), in1=xe[:, :],
                                       op0=ALU.add, op1=ALU.add).then_inc(*text_v.of("x"))
                yield
                v.wait_ge(*text_p.at(b, "mean"))
                v.tensor_tensor(cen[:, :], xt[:, :], text_bank[:, 0:NT], ALU.subtract).then_inc(*text_v.of("center"))
                yield
                v.wait_ge(*text_a.at(b, "rstd"))
                v.tensor_tensor(hn[:, :], cen[:, :], rstd[:, :], ALU.mult).then_inc(*text_v.of("scaled"))
                v.wait_ge(*text_v.at(b, "scaled"))
                v.tensor_scalar(xt[:, :], hn[:, :], col('norm_g'), col('norm_b'), ALU.mult,
                                ALU.add).then_inc(*text_v.of("x_n"))
                yield
                for i in range(LAYERS):
                    v.wait_ge(*text_p.at(b, f"mean{i}"))
                    v.tensor_tensor(cen[:, :], xt[:, :], text_bank[:, 0:NT],
                                    ALU.subtract).then_inc(*text_v.of(f"center{i}"))
                    yield
                    v.wait_ge(*text_a.at(b, f"rstd{i}"))
                    v.tensor_tensor(sq[:, :], cen[:, :], rstd[:, :], ALU.mult).then_inc(*text_v.of(f"scaled{i}"))
                    v.wait_ge(*text_v.at(b, f"scaled{i}"))
                    v.tensor_scalar(hn[:, :], sq[:, :], col('ln_g', i), col('ln_b', i), ALU.mult,
                                    ALU.add).then_inc(*text_v.of(f"h{i}"))
                    yield
                    v.wait_ge(*text_p.at(b, f"out{i}"))
                    v.scalar_tensor_tensor(out=xt[:, :], in0=text_bank[:, 256:256 + NT], scalar=col('b2', i),
                                           in1=xt[:, :], op0=ALU.add, op1=ALU.add).then_inc(*text_v.of(f"x{i}"))
                    yield

            def mix(b, p, k):
                yield
                v.wait_ge(*mix_p.at(b, "mean"))
                v.tensor_tensor(mcen[:, :], hT[:, :], mix_bank[0:64, 0:T], ALU.subtract).then_inc(*mix_v.of("center"))
                yield
                v.wait_ge(*mix_a.at(b, "rstd"))
                v.tensor_tensor(nT[:, 0, :], mcen[:, :], mrstd[:, :], ALU.mult).then_inc(*mix_v.of("n_fwd"))
                v.tensor_tensor(nT[:, 1, ::-1], mcen[:, :], mrstd[:, :], ALU.mult).then_inc(*mix_v.of("n_bwd"))
                yield
                v.wait_ge(*mix_a.at(b, "pad"))
                for j in range(TAPS):
                    for r in range(2):
                        if j == 0:
                            ins = v.tensor_scalar(pre[:, r, :], xpad[:, r, 0:T], col('conv_w', r * TAPS),
                                                  col('conv_b', r), ALU.mult, ALU.add)
                        else:
                            if r == 0:
                                v.wait_ge(*mix_v.at(b, f"conv{j - 1}"))
                            ins = v.scalar_tensor_tensor(
                                out=pre[:, r, :], in0=xpad[:, r, j:j + T], scalar=col('conv_w', r * TAPS + j),
                                in1=pre[:, r, :], op0=ALU.mult, op1=ALU.add)
                    ins.then_inc(*mix_v.of(f"conv{j}"))
                yield
                v.wait_ge(*mix_a.at(b, "gate"))
                v.tensor_scalar(gate[:, :, :], gate[:, :, :], 1.0, None, ALU.add).then_inc(*mix_v.of("gate1"))
                v.wait_ge(*mix_v.at(b, "gate1"))
                v.reciprocal(gate[:, :, :], gate[:, :, :]).then_inc(*mix_v.of("gate2"))
                v.wait_ge(*mix_v.at(b, "gate2"))
                v.tensor_tensor(act[:, :, :], pre[:, :, :], gate[:, :, :], ALU.mult).then_inc(*mix_v.of("silu"))
                yield
                v.wait_ge(*mix_a.at(b, "dt_low"))
                v.tensor_copy(bc_parts[:, :, :], xbc[:, :, :]).then_inc(*mix_v.of("bc_hi"))
                for lo, rest, part in ((64, "bc_rest", "bc_mid"), (96, "bc_last", "bc_lo")):
                    v.wait_ge(*mix_v.at(b, "bc_hi" if lo == 64 else "bc_mid"))
                    v.tensor_tensor(xbc[lo:128, :, :], xbc[lo:128, :, :], bc_parts[lo:128, :, :],
                                    ALU.subtract).then_inc(*mix_v.of(rest))
                    v.wait_ge(*mix_v.at(b, rest))
                    v.tensor_copy(bc_parts[lo:128, :, :], xbc[lo:128, :, :]).then_inc(*mix_v.of(part))
                v.wait_ge(*mix_a.at(b, "dt_log"))
                v.scalar_tensor_tensor(out=dt[:, :, :], in0=dtp[:, :, :], scalar=0.0, in1=dtl[:, :, :], op0=ALU.max,
                                       op1=ALU.add).then_inc(*mix_v.of("dt"))
                v.wait_ge(*mix_v.at(b, "dt"))
                for r, d in enumerate("fb"):
                    for n in range(NS):
                        c = r * NS + n
                        ins = v.tensor_scalar(decayed[:, r, n, 1:T], dt[:, r, 1:T], dt_cap[:, c:c + 1],
                                              a_neg[:, c:c + 1], ALU.min, ALU.mult)
                    ins.then_inc(*mix_v.of(f"dt_a_{d}"))
                v.tensor_tensor(dtx[:, :, :], dt[:, :, :], act[:, 0:2, :], ALU.mult).then_inc(*mix_v.of("dtx"))
                yield
                v.wait_ge(*mix_v.at(b, "dtx"))
                for r, d in enumerate("fb"):
                    for g in range(NS // NG):
                        v.wait_ge(*mix_p.at(b, f"b_{d}{g}"))
                        bb = row_bank[g % 2][:, 0:NG * T].rearrange("p (n t) -> p n t", n=NG)
                        v.tensor_tensor(state[:, r, g * NG:(g + 1) * NG, :],
                                        dtx[:, r:r + 1, :].to_broadcast([128, NG, T]), bb,
                                        ALU.mult).then_inc(*mix_v.of(f"b_{d}{g}"))
                    v.wait_ge(*mix_a.at(b, f"decay_{d}"))
                    v.wait_ge(*mix_v.at(b, f"b_{d}{NS // NG - 1}"))
                    h_ap = state[:, r, :, :].rearrange("p n t -> p (n t)")
                    v.tensor_tensor_scan(h_ap, decayed[:, r, :, :].rearrange("p n t -> p (n t)"), h_ap, 0.0,
                                         ALU.mult, ALU.add).then_inc(*mix_v.of(f"scan_{d}"))
                    yield
                for r, d in enumerate("fb"):
                    v.wait_ge(*mix_v.at(b, f"scan_{d}"))
                    for g in range(NS // NG):
                        v.wait_ge(*mix_p.at(b, f"c_{d}{g}"))
                        cb = row_bank[g % 2][:, 0:NG * T].rearrange("p (n t) -> p n t", n=NG)
                        hg = state[:, r, g * NG:(g + 1) * NG, :]
                        v.tensor_tensor(hg, hg, cb, ALU.mult).then_inc(*mix_v.of(f"c_{d}{g}"))
                    yield
                v.wait_ge(*mix_p.at(b, "y"))
                for r in range(2):
                    ins = v.scalar_tensor_tensor(out=yv[:, r, :], in0=act[:, r, :], scalar=col('skip_d', r),
                                                 in1=wide_bank[:, r * T:(r + 1) * T], op0=ALU.mult, op1=ALU.add)
                ins.then_inc(*mix_v.of("y_skip"))
                v.wait_ge(*mix_v.at(b, "y_skip"))
                v.tensor_tensor(yv[:, :, :], yv[:, :, :], act[:, 2:4, :], ALU.mult).then_inc(*mix_v.of("y"))
                yield
                v.wait_ge(*mix_p.at(b, "merged"))
                if not first(b, 2):
                    v.wait_ge(*att_p.at(b - 2, "out"))
                v.tensor_tensor(h2T[:, p, :], hT[:, :], mix_bank[0:64, 256:256 + T], ALU.add).then_inc(*mix_v.of("h2"))
                yield
                v.wait_ge(*mix_p.at(b, "mean2"))
                v.tensor_tensor(mcen[:, :], h2T[:, p, :], mix_bank[0:64, 0:T],
                                ALU.subtract).then_inc(*mix_v.of("center2"))
                yield
                v.wait_ge(*mix_a.at(b, "rstd2"))
                v.tensor_tensor(n2T[:, :], mcen[:, :], mrstd[:, :], ALU.mult).then_inc(*mix_v.of("n2"))
                yield
                yield

            def keys(b, p, k):
                groups = [(q, h) for q in range(2) for h in range(H)]
                v.wait_ge(*key_a.at(b, "sims"))
                v.nop(nofuse=True)
                for q, h in groups:
                    ins = v.max(topv[:, q, h, 0:8], sims[:, q * H + h, :])
                ins.then_inc(*key_v.of("top8"))
                yield
                v.wait_ge(*key_v.at(b, "top8"))
                v.nop(nofuse=True)
                for q, h in groups:
                    ins = v.match_replace(left[:, q * H + h, :], topv[:, q, h, 0:8], sims[:, q * H + h, :], LOWEST)
                ins.then_inc(*key_v.of("left"))
                yield
                v.wait_ge(*key_v.at(b, "left"))
                v.nop(nofuse=True)
                for q, h in groups:
                    ins = v.max(topv[:, q, h, 8:16], left[:, q * H + h, :])
                ins.then_inc(*key_v.of("top16"))
                yield
                v.wait_ge(*key_v.at(b, "top16"))
                v.nop(nofuse=True)
                for q, h in groups:
                    v.max_index(topi[:, q, h, 0:8], topv[:, q, h, 0:8], sims[:, q * H + h, :])
                    ins = v.max_index(topi[:, q, h, 8:16], topv[:, q, h, 8:16], left[:, q * H + h, :])
                    if (q, h) == (0, H - 1):
                        yield
                ins.then_inc(*key_v.of("index"))
                yield
                v.wait_ge(*key_v.at(b, "index"))
                v.tensor_copy(topf[:, :, :, :], topi[:, :, :, :]).then_inc(*key_v.of("index_f"))
                v.tensor_tensor(cand[:, :, 0:CA].rearrange("t h (i j) -> t h i j", i=4),
                                topv[:, 0, :, 0:4].unsqueeze(3).to_broadcast([T, H, 4, TOP]),
                                topv[:, 1, :, :].unsqueeze(2).to_broadcast([T, H, 4, TOP]),
                                ALU.add).then_inc(*key_v.of("cand_a"))
                v.tensor_tensor(cand[:, :, CA:CAND].rearrange("t h (i j) -> t h i j", i=12),
                                topv[:, 0, :, 4:16].unsqueeze(3).to_broadcast([T, H, 12, 4]),
                                topv[:, 1, :, 0:4].unsqueeze(2).to_broadcast([T, H, 12, 4]),
                                ALU.add).then_inc(*key_v.of("cand_b"))
                yield
                v.wait_ge(*key_v.at(b, "cand_b"))
                v.nop(nofuse=True)
                for h in range(H):
                    ins = v.max(best[:, h, 0:8], cand[:, h, :])
                ins.then_inc(*key_v.of("best8"))
                yield
                v.wait_ge(*key_v.at(b, "best8"))
                v.nop(nofuse=True)
                for h in range(H):
                    ins = v.match_replace(cleft[:, h, :], best[:, h, 0:8], cand[:, h, :], LOWEST)
                ins.then_inc(*key_v.of("cleft"))
                yield
                v.wait_ge(*key_v.at(b, "cleft"))
                v.nop(nofuse=True)
                for h in range(H):
                    ins = v.max(best[:, h, 8:16], cleft[:, h, :])
                ins.then_inc(*key_v.of("best16"))
                yield
                v.wait_ge(*key_v.at(b, "best16"))
                v.tensor_tensor(wraw[:, :, :], best[:, :, :], best[:, :, 0:1].to_broadcast([T, H, TOP]),
                                ALU.subtract).then_inc(*key_v.of("wraw"))
                for h in range(H):
                    v.max_index(pos[:, h, 0:8], best[:, h, 0:8], cand[:, h, :])
                    ins = v.max_index(pos[:, h, 8:16], best[:, h, 8:16], cleft[:, h, :])
                ins.then_inc(*key_v.of("pos"))
                yield
                v.wait_ge(*key_v.at(b, "pos"))
                pf = pos[:, :, :].rearrange("t h s -> t (h s)")
                v.tensor_scalar(hi_a[:, :], pf, 4, None, ALU.logical_shift_right)
                v.tensor_scalar(lo_a[:, :], pf, 15, None, ALU.bitwise_and)
                v.tensor_scalar(hi_b[:, :], pf, 2, None, ALU.logical_shift_right)
                v.tensor_scalar(lo_b[:, :], pf, 3, None, ALU.bitwise_and)
                v.tensor_scalar(late[:, :], pf, float(CA), None, ALU.is_ge).then_inc(*key_v.of("bits"))
                v.wait_ge(*key_v.at(b, "bits"))
                v.tensor_copy(fa[:, 0, :], hi_a[:, :])
                v.tensor_copy(fa[:, 1, :], lo_a[:, :])
                v.scalar_tensor_tensor(out=fb[:, 0, :], in0=hi_b[:, :], scalar=-12.0, in1=hi_a[:, :], op0=ALU.add,
                                       op1=ALU.subtract)
                v.tensor_tensor(fb[:, 1, :], lo_b[:, :], lo_a[:, :], ALU.subtract).then_inc(*key_v.of("bits_f"))
                v.wait_ge(*key_v.at(b, "bits_f"))
                v.tensor_tensor(fb[:, :, :], fb[:, :, :], late[:, :].unsqueeze(1).to_broadcast([T, 2, H * TOP]),
                                ALU.mult).then_inc(*key_v.of("ranks_a"))
                v.wait_ge(*key_v.at(b, "ranks_a"))
                v.tensor_tensor(fa[:, :, :], fa[:, :, :], fb[:, :, :], ALU.add).then_inc(*key_v.of("ranks_b"))
                yield
                v.wait_ge(*key_v.at(b, "ranks_b"))
                hit4 = hit[:, :, :].rearrange("t (h s) r -> t h s r", h=H)
                for q in range(2):
                    if q == 1:
                        v.wait_ge(*key_v.at(b, "found0"))
                    v.tensor_tensor(hit[:, :, :], fa[:, q, :].unsqueeze(2).to_broadcast([T, H * TOP, TOP]),
                                    W('iota16')[0:T].unsqueeze(1).to_broadcast([T, H * TOP, TOP]),
                                    ALU.is_equal).then_inc(*key_v.of(f"hit{q}"))
                    v.wait_ge(*key_v.at(b, f"hit{q}"))
                    v.tensor_tensor(hit4, hit4, topf[:, q, :, :].unsqueeze(2).to_broadcast([T, H, TOP, TOP]),
                                    ALU.mult).then_inc(*key_v.of(f"pick{q}"))
                    v.wait_ge(*key_v.at(b, f"pick{q}"))
                    v.tensor_reduce(found[:, q, :], hit[:, :, :], AX.X, ALU.add).then_inc(*key_v.of(f"found{q}"))
                    yield
                v.wait_ge(*key_v.at(b, "found1"))
                v.scalar_tensor_tensor(out=flat[:, :], in0=found[:, 1, :], scalar=float(NK), in1=found[:, 0, :],
                                       op0=ALU.mult, op1=ALU.add).then_inc(*key_v.of("flat"))
                v.wait_ge(*key_v.at(b, "flat"))
                v.tensor_tensor(found[:, 0, :], flat[:, :], W('head_base')[0:T], ALU.add).then_inc(*key_v.of("rows_f"))
                v.wait_ge(*key_a.at(b, "wexp"))
                v.tensor_reduce(wsum[:, :], wexp[:, :, :], AX.X, ALU.add).then_inc(*key_v.of("wsum"))
                v.wait_ge(*key_v.at(b, "wsum"))
                v.reciprocal(wrec[:, :], wsum[:, :]).then_inc(*key_v.of("wrec"))
                v.wait_ge(*key_v.at(b, "wrec"))
                v.tensor_tensor(wts[:, :].rearrange("t (h s) -> t h s", h=H), wexp[:, :, :],
                                wrec[:, :].unsqueeze(2).to_broadcast([T, H, TOP]), ALU.mult).then_inc(*key_v.of("wts"))
                yield
                v.wait_ge(*key_p.at(b, "rows_turn"))
                if not first(b, 2):
                    v.wait_ge(gathered[len(CHUNKS) - 1], (b - 1) * 16 * CHUNKS[-1])
                v.tensor_copy(rows[:, p, :], mix_bank[:, 0:T]).then_inc(*key_v.of("rows"))
                v.wait_ge(*key_p.at(b, "wts_turn"))
                if not first(b, 2):
                    v.wait_ge(*sum_p.at(b - 2, f"c{len(CHUNKS) - 1}"))
                v.tensor_tensor(spread[:, p, :, :], wide_bank[:, 0:T].unsqueeze(2).to_broadcast([PAIRS, T, H]),
                                W('own_head').unsqueeze(1).to_broadcast([PAIRS, T, H]),
                                ALU.mult).then_inc(*key_v.of("spread"))
                yield

            def sums_low(b, p, k):
                return idle(2 * SPLIT)

            def sums_high(b, p, k):
                return idle(2 * (len(CHUNKS) - SPLIT))

            def attend(b, p, k):
                yield
                v.wait_ge(*att_p.at(b, "sim"))
                for c in range(2):
                    ins = v.tensor_tensor(att[:, 4 * c:4 * c + 4, :],
                                          head_bank[c][0:T, 0:4 * T].rearrange("t (h j) -> t h j", h=4),
                                          W('causal')[0:T].unsqueeze(1).to_broadcast([T, 4, T]), ALU.add)
                ins.then_inc(*att_v.of("masked"))
                v.wait_ge(*att_v.at(b, "masked"))
                v.tensor_reduce(rmax[:, :], att[:, :, :], AX.X, ALU.max).then_inc(*att_v.of("max"))
                v.wait_ge(*att_v.at(b, "max"))
                v.tensor_tensor(att[:, :, :], att[:, :, :], rmax[:, :].unsqueeze(2).to_broadcast([T, H, T]),
                                ALU.subtract).then_inc(*att_v.of("less"))
                yield
                v.wait_ge(*att_a.at(b, "exp"))
                v.tensor_reduce(rsum[:, :], att[:, :, :], AX.X, ALU.add).then_inc(*att_v.of("sum"))
                v.wait_ge(*att_v.at(b, "sum"))
                v.reciprocal(rrec[:, :], rsum[:, :]).then_inc(*att_v.of("rec"))
                v.wait_ge(*att_v.at(b, "rec"))
                v.tensor_tensor(att[:, :, :], att[:, :, :], rrec[:, :].unsqueeze(2).to_broadcast([T, H, T]),
                                ALU.mult).then_inc(*att_v.of("probs"))
                yield
                yield

            schedule(v, text, mix, keys, sums_low, sums_high, attend)

        @block.scalar
        def _(a):
            a.wait_ge(weights_in, 32)
            a.preload_act_table_set(LOG_EXP)
            a.activation(decay_e[:, 0:1], col('decay'), ACT.Exp, scale=-1.0)
            a.wait_ge(setup_v, 1)
            a.activation(a_neg[:, :], a_neg[:, :], ACT.Exp)
            a.activation(dt_cap[:, :], dt_cap[:, :], ACT.Exp, scale=-1.0).then_inc(setup_a, 1)
            a.wait_ge(setup_v, 5)

            def stats(sig, b, cen_ap, sq_ap, lnv_ap, rstd_ap, bank_ap, centre, var_at, names):
                square, log, rstd_name = names
                parts = cen_ap.shape[0]
                a.wait_ge(*centre)
                a.activation(sq_ap, cen_ap, ACT.Square).then_inc(*sig.of(square))
                a.wait_ge(*var_at)
                a.activation(lnv_ap, bank_ap, ACT.Ln, bias=col('eps')[0:parts]).then_inc(*sig.of(log))
                a.wait_ge(*sig.at(b, log))
                a.activation(rstd_ap, lnv_ap, ACT.Exp, scale=-0.5).then_inc(*sig.of(rstd_name))

            def text_stats(b, i):
                stats(text_a, b, cen[:, :], sq[:, :], lnv[:, :], rstd[:, :], text_bank[:, 128:128 + NT],
                      text_v.at(b, f"center{i}"), text_p.at(b, f"var{i}"), (f"square{i}", f"log{i}", f"rstd{i}"))

            def mix_stats(b, i):
                stats(mix_a, b, mcen[:, :], msq[:, :], mlnv[:, :], mrstd[:, :], mix_bank[0:64, 128:128 + T],
                      mix_v.at(b, f"center{i}"), mix_p.at(b, f"var{i}"), (f"square{i}", f"log{i}", f"rstd{i}"))

            def text(b, p, k):
                a.wait_ge(*text_p.at(b, "embed"))
                a.activation(xe[:, :], text_bank[:, 0:NT], ACT.Copy).then_inc(*text_a.of("embed"))
                yield
                yield
                yield
                text_stats(b, "")
                yield
                yield
                for i in range(LAYERS):
                    text_stats(b, i)
                    yield
                    a.wait_ge(*text_p.at(b, f"hidden{i}"))
                    for c in range(FC):
                        ins = a.activation(hid[:, c, :], hidden_bank[:, c * NT:(c + 1) * NT], ACT.Gelu,
                                           bias=col('b1', i * FC + c))
                    ins.then_inc(*text_a.of(f"gelu{i}"))
                    a.preload_act_table_set(LOG_EXP)
                    yield
                    yield

            def mix(b, p, k):
                a.wait_ge(*text_p.at(b, "stream"))
                a.activation(hT[:, 0:NI], hidden_bank[0:64, 384:384 + NI], ACT.Identity, bias=scol('tok_b'))
                a.activation(hT[:, NI:T], hidden_bank[0:64, 384 + NI:384 + T], ACT.Identity,
                             bias=scol('head_b')).then_inc(*mix_a.of("stream"))
                yield
                mix_stats(b, "")
                yield
                a.wait_ge(*mix_p.at(b, "xz"))
                xz = wide_bank[:, 0:4 * T].rearrange("p (c t) -> p c t", c=4)
                a.activation(xpad[:, :, TAPS - 1:], xz[:, 0:2, :], ACT.Copy).then_inc(*mix_a.of("pad"))
                a.activation(pre[:, 2:4, :], xz[:, 2:4, :], ACT.Copy).then_inc(*mix_a.of("z"))
                yield
                a.wait_ge(*mix_a.at(b, "z"))
                a.wait_ge(*mix_v.at(b, "conv3"))
                a.activation(gate[:, :, :], pre[:, :, :], ACT.Exp, scale=-1.0).then_inc(*mix_a.of("gate"))
                yield
                a.wait_ge(*mix_p.at(b, "dt_low"))
                a.activation(xbc[:, :, :], mix_bank[:, 0:2 * T].rearrange("p (r t) -> p r t", r=2),
                             ACT.Copy).then_inc(*mix_a.of("dt_low"))
                a.wait_ge(*mix_p.at(b, "dt_pre"))
                for r in range(2):
                    ins = a.activation(dtp[:, r, :], mix_bank[:, 256 + r * T:256 + (r + 1) * T], ACT.Identity,
                                       bias=col('b_dt', r))
                ins.then_inc(*mix_a.of("dt_pre"))
                a.wait_ge(*mix_a.at(b, "dt_pre"))
                a.activation(dte[:, :, :], dtp[:, :, :], ACT.Abs).then_inc(*mix_a.of("abs"))
                a.wait_ge(*mix_a.at(b, "abs"))
                a.activation(dtl[:, :, :], dte[:, :, :], ACT.Exp, scale=-1.0).then_inc(*mix_a.of("exp"))
                a.wait_ge(*mix_a.at(b, "exp"))
                a.activation(dtl[:, :, :], dtl[:, :, :], ACT.Ln, bias=1.0).then_inc(*mix_a.of("dt_log"))
                yield
                for r, d in enumerate("fb"):
                    a.wait_ge(*mix_v.at(b, f"dt_a_{d}"))
                    a.activation(decayed[:, r, :, 1:T], decayed[:, r, :, 1:T],
                                 ACT.Exp).then_inc(*mix_a.of(f"decay_{d}"))
                yield
                yield
                yield
                yield
                yield
                a.wait_ge(*mix_p.at(b, "o"))
                a.activation(oT[:, 0, :], mix_bank[0:64, 0:T], ACT.Copy)
                a.activation(oT[:, 1, ::-1], mix_bank[0:64, T:2 * T], ACT.Copy).then_inc(*mix_a.of("o"))
                yield
                yield
                mix_stats(b, 2)
                yield
                a.wait_ge(*key_p.at(b, "q"))
                a.activation(qp[:, :, :], wide_bank[:, 0:4 * T].rearrange("p (c t) -> p c t", c=4),
                             ACT.Copy).then_inc(*key_a.of("q"))
                yield
                a.wait_ge(*key_p.at(b, "sims"))
                if not first(b):
                    a.wait_ge(*key_v.at(b - 1, "index"))
                for c in range(2):
                    ins = a.activation(sims[:, c * H:(c + 1) * H, :],
                                       row_bank[c][0:T, :].rearrange("t (h k) -> t h k", h=H), ACT.Copy)
                ins.then_inc(*key_a.of("sims"))
                a.wait_ge(*key_p.at(b, "heads"))
                if not first(b, 2):
                    a.wait_ge(*att_p.at(b - 2, "sim"))
                for c in range(2):
                    ins = a.activation(qT[:, p, 4 * c:4 * c + 4, :],
                                       (mix_bank, wide_bank)[c][0:64, 0:4 * T].rearrange("d (h t) -> d h t", h=4),
                                       ACT.Copy, scale=float(E) ** -0.5)
                ins.then_inc(*key_a.of("heads"))
                yield

            def keys(b, p, k):
                for _ in range(9):
                    yield
                a.wait_ge(*key_v.at(b, "wraw"))
                a.activation(wexp[:, :, :], wraw[:, :, :], ACT.Exp).then_inc(*key_a.of("wexp"))
                for _ in range(6):
                    yield

            def copy_sums(b, chunks):
                for c in chunks:
                    yield
                    if c in (HALF - 1, len(CHUNKS) - 1):
                        half = c // HALF
                        t0, t1 = half * BANK_TOKENS, min(T, (half + 1) * BANK_TOKENS)
                        a.wait_ge(*sum_p.at(b, f"c{c}"))
                        if half == 0 and not first(b):
                            a.wait_ge(*att_p.at(b - 1, "vw"))
                        a.activation(kvT[:, :, t0:t1],
                                     head_bank[half][:, 0:(t1 - t0) * H].rearrange("p (t h) -> p h t", h=H),
                                     ACT.Copy).then_inc(*sum_a.of(("low", "high")[half]))
                    yield

            def sums_low(b, p, k):
                return copy_sums(b, range(SPLIT))

            def sums_high(b, p, k):
                return copy_sums(b, range(SPLIT, len(CHUNKS)))

            def attend(b, p, k):
                yield
                a.wait_ge(*att_v.at(b, "less"))
                a.activation(att[:, :, :], att[:, :, :], ACT.Exp).then_inc(*att_a.of("exp"))
                a.wait_ge(*att_p.at(b, "vw"))
                a.activation(vw[:, :, :], head_bank[0][0:T, :].rearrange("t (h e) -> t h e", h=H),
                             ACT.Copy).then_inc(*att_a.of("vw"))
                yield
                a.wait_ge(*att_p.at(b, "turn"))
                for c in range(2):
                    ins = a.activation(attT[:, 4 * c:4 * c + 4, :],
                                       head_bank[c][0:T, 0:4 * T].rearrange("t (h j) -> t h j", h=4), ACT.Copy)
                ins.then_inc(*att_a.of("turn"))
                yield
                a.wait_ge(*att_p.at(b, "out"))
                if not first(b, 2):
                    a.wait_ge(out_sent[p], k * 16)
                a.activation(res[:, p, :], head_bank[0][0:T, 0:E], ACT.Copy).then_inc(*att_a.of("out"))
                a.wait_ge(*att_a.at(b, "out"))
                a.dma_start(out[b], res[:, p, :]).then_inc(out_sent[p], 16)
                yield

            schedule(a, text, mix, keys, sums_low, sums_high, attend)
            for p in range(2):
                a.wait_ge(out_sent[p], 16 * B // 2)

        @block.tensor
        def _(t):
            t.wait_ge(weights_in, 32)

            def mm(o, lhsT, rhs, start=True, stop=True):
                return t.matmul(o, lhsT, rhs, start=start, stop=stop)

            def text(b, p, k):
                t.wait_ge(*text_v.at(b, "onehot"))
                mm(text_bank[:, 0:NT], S('emb'), onehot[:, :]).then_inc(*text_p.of("embed"))
                t.wait_ge(*text_a.at(b, "embed"))
                mm(text_bank[:, 128:128 + NT], W('w_upd'), xe[:, :]).then_inc(*text_p.of("u"))
                yield
                t.wait_ge(*text_v.at(b, "mems"))
                mm(text_bank[:, 256:256 + NT], W('w_f'), mems[:, :]).then_inc(*text_p.of("f"))
                yield

                def mean(i, ready):
                    t.wait_ge(*text_v.at(b, ready))
                    mm(text_bank[:, 0:NT], W('mean128'), xt[:, :]).then_inc(*text_p.of(f"mean{i}"))

                def var(i):
                    t.wait_ge(*text_v.at(b, f"center{i}"))
                    t.wait_ge(*text_a.at(b, f"square{i}"))
                    mm(text_bank[:, 128:128 + NT], W('mean128'), sq[:, :]).then_inc(*text_p.of(f"var{i}"))

                mean("", "x")
                yield
                var("")
                yield
                mean(0, "x_n")
                yield
                for i in range(LAYERS):
                    var(i)
                    yield
                    t.wait_ge(*text_v.at(b, f"h{i}"))
                    if i == 0 and not first(b):
                        t.wait_ge(*mix_a.at(b - 1, "stream"))
                    for c in range(FC):
                        ins = mm(hidden_bank[:, c * NT:(c + 1) * NT], w1[:, i, c, :], hn[:, :])
                    ins.then_inc(*text_p.of(f"hidden{i}"))
                    t.wait_ge(*text_a.at(b, f"gelu{i}"))
                    for c in range(FC):
                        ins = mm(text_bank[:, 256:256 + NT], w2[:, i, c, :], hid[:, c, :], c == 0, c == FC - 1)
                    ins.then_inc(*text_p.of(f"out{i}"))
                    yield
                    if i < LAYERS - 1:
                        mean(i + 1, f"x{i}")
                        yield
                t.wait_ge(x_in[p], (k + 1) * 16)
                for c in range(KC):
                    mm(hidden_bank[0:64, 384:384 + NI], tok_w[:, c, :], xin[:, p, c, :], c == 0, c == KC - 1)
                t.wait_ge(*text_v.at(b, f"x{LAYERS - 1}"))
                mm(hidden_bank[0:64, 384 + NI:384 + T], W('head_w'), xt[:, :]).then_inc(*text_p.of("stream"))
                yield

            def mix(b, p, k):
                def mean(i, x_ap, ready):
                    t.wait_ge(*ready)
                    t.nop(nofuse=True)
                    mm(mix_bank[0:64, 0:T], S('mean64'), x_ap).then_inc(*mix_p.of(f"mean{i}"))

                def var(i):
                    t.wait_ge(*mix_v.at(b, f"center{i}"))
                    t.wait_ge(*mix_a.at(b, f"square{i}"))
                    t.nop(nofuse=True)
                    mm(mix_bank[0:64, 128:128 + T], S('mean64'), msq[:, :]).then_inc(*mix_p.of(f"var{i}"))

                if not first(b):
                    t.wait_ge(*key_v.at(b - 1, "spread"))
                mean("", hT[:, :], mix_a.at(b, "stream"))
                yield
                var("")
                yield
                t.wait_ge(*mix_v.at(b, "n_bwd"))
                for z in range(2):
                    for r in range(2):
                        o = (2 * z + r) * T
                        ins = mm(wide_bank[:, o:o + T], w_in[:, r, z, :], nT[:, r, :])
                ins.then_inc(*mix_p.of("xz"))
                yield
                yield
                t.wait_ge(*mix_v.at(b, "silu"))
                for r in range(2):
                    ins = mm(mix_bank[:, r * T:(r + 1) * T], w_x[:, r, :], act[:, r, :])
                ins.then_inc(*mix_p.of("dt_low"))
                t.wait_ge(*mix_a.at(b, "dt_low"))
                for r in range(2):
                    ins = mm(mix_bank[:, 256 + r * T:256 + (r + 1) * T], w_dt[:, r, :], xbc[0:RK, r, :])
                ins.then_inc(*mix_p.of("dt_pre"))
                t.wait_ge(*mix_v.at(b, "bc_lo"))
                t.nop(nofuse=True)
                names = [(m, r, g) for m in range(2) for r in range(2) for g in range(NS // NG)]

                def name(c):
                    m, r, g = names[c]
                    return f"{'bc'[m]}_{'fb'[r]}{g}"

                def row_group(c):
                    m, r, g = names[c]
                    if c >= 2:
                        t.wait_ge(*mix_v.at(b, name(c - 2)))
                    for n in range(NG):
                        w = m * NS + g * NG + n
                        ins = mm(row_bank[g % 2][:, n * T:(n + 1) * T],
                                 own_row[:, w:w + 1].to_broadcast([128, 128]), bc_parts[:, r, :])
                    ins.then_inc(*mix_p.of(name(c)))

                if not first(b):
                    t.wait_ge(*key_a.at(b - 1, "sims"))
                row_group(0)
                row_group(1)
                yield
                yield
                for c in range(2, 6):
                    row_group(c)
                yield
                for c in range(6, 10):
                    row_group(c)
                yield

                def sum_states(r):
                    for n in range(NS):
                        if n % NG == 0:
                            t.wait_ge(*mix_v.at(b, f"c_{'fb'[r]}{n // NG}"))
                        ins = mm(wide_bank[:, r * T:(r + 1) * T], ident, state[:, r, n, :], n == 0, n == NS - 1)
                    return ins

                for c in range(10, 14):
                    row_group(c)
                yield
                row_group(14)
                row_group(15)
                sum_states(0)
                sum_states(1).then_inc(*mix_p.of("y"))
                yield
                t.wait_ge(*mix_v.at(b, "y"))
                for r in range(2):
                    ins = mm(mix_bank[0:64, r * T:(r + 1) * T], w_out[:, r, :], yv[:, r, :])
                ins.then_inc(*mix_p.of("o"))
                t.wait_ge(*mix_a.at(b, "o"))
                t.nop(nofuse=True)
                for r in range(2):
                    ins = mm(mix_bank[0:64, 256:256 + T], merge[:, r, :], oT[:, r, :], r == 0, r == 1)
                ins.then_inc(*mix_p.of("merged"))
                yield
                mean(2, h2T[:, p, :], mix_v.at(b, "h2"))
                yield
                var(2)
                yield
                t.wait_ge(*mix_v.at(b, "n2"))
                for c in range(4):
                    ins = mm(wide_bank[:, c * T:(c + 1) * T], wq_pk[:, c, :], n2T[:, :])
                ins.then_inc(*key_p.of("q"))
                yield
                t.wait_ge(*key_a.at(b, "q"))
                for c in range(4):
                    o = 256 * (c % 2)
                    ins = mm(row_bank[c // 2][0:T, o:o + 256], qp[:, c, :], pk_keys[:, c, :])
                ins.then_inc(*key_p.of("sims"))
                for h in range(H):
                    o = (h % 4) * T
                    ins = mm((mix_bank, wide_bank)[h // 4][0:64, o:o + T], wq[:, h, :], n2T[:, :])
                ins.then_inc(*key_p.of("heads"))
                yield

            def keys(b, p, k):
                for _ in range(13):
                    yield
                t.wait_ge(*key_v.at(b, "rows_f"))
                t.wait_ge(*key_a.at(b, "heads"))
                t.nop(nofuse=True)
                t.transpose(mix_bank[:, 0:T], found[:, 0, :], ident[0:T, 0:T]).then_inc(*key_p.of("rows_turn"))
                t.wait_ge(*key_v.at(b, "wts"))
                t.nop(nofuse=True)
                t.transpose(wide_bank[:, 0:T], wts[:, :], ident[0:T, 0:T]).then_inc(*key_p.of("wts_turn"))
                yield
                yield

            def add_rows(b, p, chunks):
                for c in chunks:
                    if c == 0:
                        t.wait_ge(*key_v.at(b, "spread"))
                        if not first(b):
                            t.wait_ge(*att_a.at(b - 1, "out"))
                    t.wait_ge(gathered[c], (b + 1) * 16 * CHUNKS[c])
                    t.nop(nofuse=True)
                    for j in range(STARTS[c], STARTS[c] + CHUNKS[c]):
                        if j == STARTS[c] + CHUNKS[c] // 2:
                            yield
                        o = j % BANK_TOKENS * H
                        n = min(BUSY_TOKENS, BANK_TOKENS - j % BANK_TOKENS, T - j)
                        ins = mm(head_bank[j // BANK_TOKENS][:, o:o + n * H], G[:, j, :],
                                 spread[:, p, j:j + n, :].rearrange("p t h -> p (t h)"))
                    ins.then_inc(*sum_p.of(f"c{c}"))
                    yield

            def sums_low(b, p, k):
                return add_rows(b, p, range(SPLIT))

            def sums_high(b, p, k):
                return add_rows(b, p, range(SPLIT, len(CHUNKS)))

            def attend(b, p, k):
                t.wait_ge(*sum_a.at(b, "high"))
                t.nop(nofuse=True)
                for h in range(H):
                    o = (h % 4) * T
                    ins = mm(head_bank[h // 4][0:T, o:o + T], qT[:, p, h, :], kvT[0:E, h, :])
                ins.then_inc(*att_p.of("sim"))
                yield
                t.wait_ge(*att_v.at(b, "masked"))
                t.nop(nofuse=True)
                for h in range(H):
                    ins = mm(head_bank[0][0:T, h * E:(h + 1) * E], kvT[E:KV, h, :], wo[E:KV, h, :])
                ins.then_inc(*att_p.of("vw"))
                yield
                t.wait_ge(*att_v.at(b, "probs"))
                t.wait_ge(*att_a.at(b, "vw"))
                t.nop(nofuse=True)
                for h in range(H):
                    o = (h % 4) * T
                    ins = t.transpose(head_bank[h // 4][0:T, o:o + T], att[:, h, :], ident[0:T, 0:T])
                ins.then_inc(*att_p.of("turn"))
                yield
                t.wait_ge(*att_a.at(b, "turn"))
                t.nop(nofuse=True)
                for h in range(H):
                    mm(head_bank[0][0:T, 0:E], attT[:, h, :], vw[:, h, :], h == 0, False)
                mm(head_bank[0][0:T, 0:E], h2T[:, p, :], ident[0:64, 0:64], False, True).then_inc(*att_p.of("out"))
                yield

            schedule(t, text, mix, keys, sums_low, sums_high, attend)


def kernel(**inputs):
    import concourse.bacc as bacc
    from concourse.bass_utils import run_bass_kernel_spmd

    a = {name: np.asarray(value) for name, value in inputs.items()}

    def txt(name):
        return a['L0_txt_' + name]

    def both(name):
        return np.stack([a[f'L0_attn_{d}_{name}'] for d in ('fw', 'bw')])

    def rows128(w):
        return w.reshape(-1, 128, w.shape[-1]).transpose(1, 0, 2).reshape(128, -1)

    pk = a['L0_ffn_pk_keys']
    blocks = np.zeros((4, 32, 4, 4, NK), np.float32)
    for c in range(4):
        for j in range(4):
            blocks[j, :, c, j, :] = pk[c // 2, :, (c % 2) * 4 + j, :].T
    tri = np.where(np.tril(np.ones((T, T), bool)), 0.0, LOWEST).astype(np.float32)
    causal = np.zeros((128, T), np.float32)
    causal[0:T] = tri
    w_x = np.zeros((2, DM, 128), np.float32)
    w_x[:, :, 0:RK] = both('W_x')[:, :, 0:RK]
    w_x[:, :, 32:128] = np.tile(both('W_x')[:, :, RK:], (1, 1, 3))
    own_row = np.tile(np.eye(2 * NS, dtype=np.float32), (4, 1))
    own_row[0:32] = 0.0
    wide = {
        'ident': np.eye(128, dtype=np.float32), 'mean128': np.full((128, 128), 1.0 / 128, np.float32),
        'w_upd': txt('W_upd'), 'w_f': txt('W_f'),
        'w1': txt('cms_W1').transpose(1, 0, 2).reshape(128, -1),
        'w2': rows128(txt('cms_W2').reshape(-1, 128)),
        'head_w': txt('head_W'), 'tok_w': rows128(a['L0_tok_W'].T),
        'ln_g': txt('cms_ln_g').T, 'ln_b': txt('cms_ln_b').T, 'b1': txt('cms_b1').reshape(-1, 128).T,
        'b2': txt('cms_b2').T, 'w_x': w_x.transpose(1, 0, 2).reshape(128, -1),
        'w_out': both('W_out').transpose(1, 0, 2).reshape(128, -1),
        'conv_w': both('conv_w').transpose(1, 0, 2).reshape(128, -1),
        'conv_b': both('conv_b').T, 'b_dt': both('b_dt').T,
        'a_log': both('A_log').transpose(1, 0, 2).reshape(128, -1), 'skip_d': both('D').T,
        'pk_keys': blocks.reshape(128, -1), 'causal': causal,
        'iota16': np.broadcast_to(np.arange(TOP, dtype=np.float32), (128, TOP)),
        'own_row': own_row, 'own_head': np.repeat(np.eye(H, dtype=np.float32), TOP, axis=0),
        'wo': np.tile(a['L0_ffn_Wo'].reshape(H, 64, 64).transpose(1, 0, 2).reshape(64, -1), (2, 1)),
        'head_base': np.broadcast_to(np.repeat(np.arange(H, dtype=np.float32) * NK * NK, TOP), (128, H * TOP)),
        'b_upd': txt('b_upd')[:, None], 'b_f': txt('b_f')[:, None], 'norm_g': txt('norm_g')[:, None],
        'norm_b': txt('norm_b')[:, None], 'decay': np.broadcast_to(txt('decay_param'), (128, 1)),
        'eps': np.full((128, 1), EPS, np.float32), 'iota': np.arange(128, dtype=np.float32)[:, None],
    }
    w_dt = np.zeros((64, 2 * DM), np.float32)
    w_dt[0:RK] = both('W_dt').transpose(1, 0, 2).reshape(RK, -1)
    slim = {
        'emb': txt('emb'), 'mean64': np.full((64, 64), 1.0 / 64, np.float32),
        'w_in': both('W_in').transpose(1, 0, 2).reshape(64, -1), 'w_dt': w_dt,
        'merge': a['L0_attn_merge_W'].reshape(2, 64, 64).transpose(1, 0, 2).reshape(64, -1),
        'wq_pk': a['L0_ffn_Wq_pk'], 'wq': a['L0_ffn_Wq'],
        'tok_b': a['L0_tok_b'][:, None], 'head_b': txt('head_b')[:, None],
    }
    patches = a['x'].reshape(B, 3, 6, 16, 6, 16).transpose(0, 1, 3, 5, 2, 4).reshape(B, KC, 128, NI)
    arrays = {
        'patches': patches.transpose(0, 2, 1, 3), 'tokens': a['x_txt'],
        'wide_w': np.concatenate([wide[n] for n, _ in WIDE], axis=1),
        'slim_w': np.concatenate([slim[n] for n, _ in SLIM], axis=1),
        'table': np.concatenate([a['L0_ffn_keys_table'], a['L0_ffn_values_table']], axis=1),
    }
    arrays = {name: np.ascontiguousarray(value) for name, value in arrays.items()}
    nc = bacc.Bacc("TRN2", target_bir_lowering=False, num_devices=1)
    args = [nc.dram_tensor(name, v.shape, mybir.dt.from_np(v.dtype), kind="ExternalInput").ap()
            for name, v in arrays.items()]
    out = nc.dram_tensor("fused", (B, T, E), F32, kind="ExternalOutput").ap()
    fused_embed_kernel(nc, *args, out)
    r = run_bass_kernel_spmd(nc, [arrays], core_ids=[0])
    return r.results[0]["fused"]
```
